# Optimizing a Trainium2 kernel written in Bass

```python
import numpy as np
import jax
import jax.numpy as jnp

def _softmax(x, axis=-1):
    return jax.nn.softmax(x, axis=axis)

def _gelu(x):
    return jax.nn.gelu(x, approximate=True)

def _silu(x):
    return jax.nn.silu(x)

def _sigmoid(x):
    return jax.nn.sigmoid(x)

def _layernorm(x, axis=-1, eps=1e-05):
    m = jnp.mean(x, axis=axis, keepdims=True)
    v = jnp.var(x, axis=axis, keepdims=True)
    return (x - m) / jnp.sqrt(v + eps)

def _scatter_add(tgt, idx, src, axis=0):
    return tgt.at[idx].add(src)

def _segment_sum(src, seg, n):
    return jax.ops.segment_sum(src, seg, n)
kernel_name = 'mk_cond_resid_d4_seqx_r8_d51918'

def setup_inputs(seed: int=0):
    np.random.seed(seed)
    _w = jnp.asarray

    def _rec_inputs():
        import jax
        import jax.numpy as jnp
        _rk = jax.random.key(seed)
        x = -0.000125 + 0.9999 * jax.random.normal(jax.random.fold_in(_rk, 1), (8, 128, 512), jnp.float32)
        _lenS = 128 - jax.random.randint(jax.random.fold_in(_rk, 7), (8,), 0, max(1, 128 // 4) + 1, jnp.int32)
        _lenS2 = 128 - jax.random.randint(jax.random.fold_in(_rk, 8), (8,), 0, max(1, 128 // 4) + 1, jnp.int32)
        itok_B_0_7 = jax.random.randint(jax.random.fold_in(_rk, 11), (8,), 0, 8, jnp.int32)
        condB_codebook = -0.0625 + 0.715345 * jax.random.normal(jax.random.fold_in(_rk, 12), (8,), jnp.float32)
        itok_B_2_6 = jax.random.randint(jax.random.fold_in(_rk, 13), (8,), 2, 7, jnp.int32)
        itok_B_3_7 = jax.random.randint(jax.random.fold_in(_rk, 14), (8,), 3, 8, jnp.int32)
        return (x, itok_B_0_7, condB_codebook, itok_B_2_6, itok_B_3_7)
    x, itok_B_0_7, condB_codebook, itok_B_2_6, itok_B_3_7 = _rec_inputs()

    def _L0_cond_setup():
        import jax, jax.numpy as jnp
        import numpy as np
        TOP_K = 2
        LANG_BIAS = 5.0
        SCALING = 32.0 / 16.0
        LANGUAGE_PAD_ID = -1
        key = jax.random.key(seed)
        ks = jax.random.split(key, 6)
        B, T, D, O, E, R = (4, 256, 512, 512, 8, 16)
        x = jax.random.normal(ks[0], (B, T, D), dtype=jnp.float32)
        language_ids = jax.random.randint(ks[1], (B,), 0, E).astype(jnp.int64)
        W = jax.random.normal(ks[2], (O, D), dtype=jnp.float32) * (1.0 / np.sqrt(D))
        Wr = jax.random.normal(ks[3], (E, D), dtype=jnp.float32) * (1.0 / np.sqrt(D))
        A = jax.random.normal(ks[4], (E, R, D), dtype=jnp.float32) * (1.0 / np.sqrt(D))
        Bm = jax.random.normal(ks[5], (O, R), dtype=jnp.float32) * 0.0
        Bm = jnp.broadcast_to(Bm, (E, O, R)) + jax.random.normal(ks[5], (E, O, R), dtype=jnp.float32) * 0.02
        return {'x': x, 'language_ids': language_ids, 'W': W, 'Wr': Wr, 'A': A, 'B': Bm}
    _L0_cond_all = _L0_cond_setup()
    _L0_cond_in = {k: v for k, v in _L0_cond_all.items() if k in ('W', 'Wr', 'A', 'B')}
    del _L0_cond_all

    def _L1_cond_setup():
        import jax, jax.numpy as jnp
        import numpy as np
        GROUP = 128
        LORA_ALPHA = 32.0
        LORA_RANK = 64
        key = jax.random.key(seed)
        k1, k2, k3, k4 = jax.random.split(key, 4)
        O, I = (512, 512)
        x = jax.random.normal(k1, (4, 256, I), dtype=jnp.float32)
        weight = jax.random.normal(k2, (O, I), dtype=jnp.float32) * 0.02
        wg = weight.reshape(O, I // GROUP, GROUP)
        scale_log = jnp.log(jnp.clip(jnp.max(jnp.abs(wg), axis=2, keepdims=True), 1e-05))
        codebook = jnp.array([-1.0, -0.25, 0.0, 1.0], dtype=jnp.float32)
        lora_A = jax.random.normal(k3, (LORA_RANK, I), dtype=jnp.float32) * 0.02
        lora_B = jax.random.normal(k4, (O, LORA_RANK), dtype=jnp.float32) * 0.02
        return {'x': x, 'weight': weight, 'scale_log': scale_log, 'codebook': codebook, 'lora_A': lora_A, 'lora_B': lora_B}
    _L1_cond_all = _L1_cond_setup()
    _L1_cond_in = {k: v for k, v in _L1_cond_all.items() if k in ('weight', 'scale_log', 'lora_A', 'lora_B')}
    del _L1_cond_all

    def _L2_cond_setup():
        import jax, jax.numpy as jnp
        import numpy as np
        B, N, H, F = (4, 64, 512, 1376)
        L, R, RANK = (1, 16, 16)
        SCALE = 0.5
        key = jax.random.key(seed)
        ks = jax.random.split(key, 12)
        nrm = lambda k, shape, fan: jax.random.normal(k, shape, jnp.float32) * fan ** (-0.5)
        inp = {'x': jax.random.normal(ks[0], (B, N, H), jnp.float32), 'W_gate': nrm(ks[1], (F, H), H), 'W_up': nrm(ks[2], (F, H), H), 'W_down': nrm(ks[3], (H, F), F), 'A_gate': nrm(ks[4], (L, R, RANK, H), H), 'B_gate': nrm(ks[5], (L, R, F, RANK), RANK), 'A_up': nrm(ks[6], (L, R, RANK, H), H), 'B_up': nrm(ks[7], (L, R, F, RANK), RANK), 'A_down': nrm(ks[8], (L, R, RANK, F), F), 'B_down': nrm(ks[9], (L, R, H, RANK), RANK), 'lora_indices': jax.random.randint(ks[10], (B,), 0, R), 'layer_idx': 0}
        return inp
    _L2_cond_all = _L2_cond_setup()
    _L2_cond_in = {k: v for k, v in _L2_cond_all.items() if k in ('W_gate', 'W_up', 'W_down', 'A_gate', 'B_gate', 'A_up', 'B_up', 'A_down', 'B_down')}
    del _L2_cond_all

    def _L3_cond_setup():
        import jax, jax.numpy as jnp
        import numpy as np
        RANK = 16
        ALPHA = 16.0
        SCALING = ALPHA / RANK
        N_ADAPTERS = 8
        IN_F = 512
        OUT_F = 512
        BATCH = 4
        SEQ = 256
        key = jax.random.key(seed)
        kx, ka, kb, ki = jax.random.split(key, 4)
        x = jax.random.normal(kx, (BATCH, SEQ, IN_F), dtype=jnp.float32)
        A = jax.random.normal(ka, (N_ADAPTERS, OUT_F, RANK), dtype=jnp.float32) * 0.02
        B = jax.random.normal(kb, (N_ADAPTERS, RANK, IN_F), dtype=jnp.float32) * 0.02
        adapter_ids = jax.random.randint(ki, (BATCH,), 0, N_ADAPTERS, dtype=jnp.int32)
        return {'x': x, 'A': A, 'B': B, 'adapter_ids': adapter_ids}
    _L3_cond_all = _L3_cond_setup()
    _L3_cond_in = {k: v for k, v in _L3_cond_all.items() if k in ('A', 'B')}
    del _L3_cond_all
    return {'x': x, 'itok_B_0_7': itok_B_0_7, 'condB_codebook': condB_codebook, 'itok_B_2_6': itok_B_2_6, 'itok_B_3_7': itok_B_3_7, 'L0_cond_W': _L0_cond_in['W'], 'L0_cond_Wr': _L0_cond_in['Wr'], 'L0_cond_A': _L0_cond_in['A'], 'L0_cond_B': _L0_cond_in['B'], 'L1_cond_weight': _L1_cond_in['weight'], 'L1_cond_scale_log': _L1_cond_in['scale_log'], 'L1_cond_lora_A': _L1_cond_in['lora_A'], 'L1_cond_lora_B': _L1_cond_in['lora_B'], 'L2_cond_W_gate': _L2_cond_in['W_gate'], 'L2_cond_W_up': _L2_cond_in['W_up'], 'L2_cond_W_down': _L2_cond_in['W_down'], 'L2_cond_A_gate': _L2_cond_in['A_gate'], 'L2_cond_B_gate': _L2_cond_in['B_gate'], 'L2_cond_A_up': _L2_cond_in['A_up'], 'L2_cond_B_up': _L2_cond_in['B_up'], 'L2_cond_A_down': _L2_cond_in['A_down'], 'L2_cond_B_down': _L2_cond_in['B_down'], 'L3_cond_A': _L3_cond_in['A'], 'L3_cond_B': _L3_cond_in['B']}

def reference(x, itok_B_0_7, condB_codebook, itok_B_2_6, itok_B_3_7, L0_cond_W, L0_cond_Wr, L0_cond_A, L0_cond_B, L1_cond_weight, L1_cond_scale_log, L1_cond_lora_A, L1_cond_lora_B, L2_cond_W_gate, L2_cond_W_up, L2_cond_W_down, L2_cond_A_gate, L2_cond_B_gate, L2_cond_A_up, L2_cond_B_up, L2_cond_A_down, L2_cond_B_down, L3_cond_A, L3_cond_B):
    import jax
    import jax.numpy as jnp

    def _L0_cond_ref(x, language_ids, W, Wr, A, B):
        import jax, jax.numpy as jnp
        import numpy as np
        TOP_K = 2
        LANG_BIAS = 5.0
        SCALING = 32.0 / 16.0
        LANGUAGE_PAD_ID = -1
        base = jnp.einsum('btd,od->bto', x, W)
        E = Wr.shape[0]
        logits = jnp.einsum('btd,ed->bte', x.astype(jnp.float32), Wr.astype(jnp.float32))
        expert_targets = language_ids
        valid = expert_targets >= 0
        tgt = jnp.where(valid, expert_targets, 0)
        bias = jax.nn.one_hot(tgt, E, dtype=logits.dtype) * LANG_BIAS
        bias = jnp.where(valid[:, None], bias, 0.0)
        logits = logits + bias[:, None, :]
        topw, topi = jax.lax.top_k(logits, TOP_K)
        weights = jax.nn.softmax(topw, axis=-1)
        gates = jnp.sum(jax.nn.one_hot(topi, E, dtype=weights.dtype) * weights[..., None], axis=-2)
        gates = gates.astype(x.dtype)
        h = jnp.einsum('btd,erd->bter', x, A)
        lora_out = jnp.einsum('bter,bte,eor->bto', h, gates, B)
        return base + SCALING * lora_out

    def _L1_cond_ref(x, weight, scale_log, codebook, lora_A, lora_B):
        import jax, jax.numpy as jnp
        import numpy as np
        GROUP = 128
        LORA_ALPHA = 32.0
        LORA_RANK = 64
        O, I = weight.shape
        lora_delta = lora_B @ lora_A * (LORA_ALPHA / LORA_RANK)
        cb = codebook / jnp.clip(jnp.max(jnp.abs(codebook)), 1e-08)
        scale = jnp.exp(scale_log)
        wg = (weight + lora_delta).reshape(O, I // GROUP, GROUP)
        normalized = wg / scale
        thresholds = (cb[:-1] + cb[1:]) * 0.5
        idx = jnp.searchsorted(thresholds, normalized, side='left')
        quantized = cb[idx]
        w = jax.lax.stop_gradient(quantized - normalized) + normalized
        w_q = (w * scale).reshape(O, I)
        w_eff = w_q + lora_delta
        return x @ w_eff.T

    def _L2_cond_ref(x, W_gate, W_up, W_down, A_gate, B_gate, A_up, B_up, A_down, B_down, lora_indices, layer_idx):
        import jax, jax.numpy as jnp
        import numpy as np
        B, N, H, F = (4, 64, 512, 1376)
        L, R, RANK = (1, 16, 16)
        SCALE = 0.5

        def lora_add(base, inp, A, B):
            Ab = A[layer_idx][lora_indices]
            Bb = B[layer_idx][lora_indices]
            t = jnp.einsum('bri,bni->bnr', Ab, inp)
            return base + jnp.einsum('bor,bnr->bno', Bb, t) * SCALE
        gate = lora_add(jnp.einsum('bnh,fh->bnf', x, W_gate), x, A_gate, B_gate)
        up = lora_add(jnp.einsum('bnh,fh->bnf', x, W_up), x, A_up, B_up)
        act = jax.nn.silu(gate) * up
        down = lora_add(jnp.einsum('bnf,hf->bnh', act, W_down), act, A_down, B_down)
        return down

    def _L3_cond_ref(x, A, B, adapter_ids):
        import jax, jax.numpy as jnp
        import numpy as np
        RANK = 16
        ALPHA = 16.0
        SCALING = ALPHA / RANK
        N_ADAPTERS = 8
        IN_F = 512
        OUT_F = 512
        BATCH = 4
        SEQ = 256
        B_sel = B[adapter_ids]
        A_sel = A[adapter_ids]
        Bx = jnp.einsum('bni,bri->bnr', x, B_sel)
        out = jnp.einsum('bnr,bor->bno', Bx, A_sel)
        return out * SCALING
    x = x + _L0_cond_ref(x, itok_B_0_7, L0_cond_W, L0_cond_Wr, L0_cond_A, L0_cond_B)
    x = x + _L1_cond_ref(x, L1_cond_weight, L1_cond_scale_log, condB_codebook, L1_cond_lora_A, L1_cond_lora_B)
    x = x + _L2_cond_ref(x, L2_cond_W_gate, L2_cond_W_up, L2_cond_W_down, L2_cond_A_gate, L2_cond_B_gate, L2_cond_A_up, L2_cond_B_up, L2_cond_A_down, L2_cond_B_down, itok_B_2_6, 0)
    x = x + _L3_cond_ref(x, L3_cond_A, L3_cond_B, itok_B_3_7)
    return x

_drawn_inputs = setup_inputs


def setup_inputs(seed=0):
    import zlib

    import numpy as np

    out = dict(_drawn_inputs(seed))
    spreads = {}
    factors = {'L0_cond_Wr': 4.213}
    for name, (base, spread) in spreads.items():
        noise = np.random.default_rng([zlib.crc32(name.encode()), seed]).standard_normal(out[name].shape)
        drawn = base * np.exp(spread * noise) if base else spread * noise
        out[name] = jnp.asarray(drawn.astype(out[name].dtype))
    for name, factor in factors.items():
        out[name] = (out[name] * factor).astype(out[name].dtype)
    return out
```

```python
from contextlib import ExitStack

import concourse.bass as bass
from concourse import mybir

ALU = mybir.AluOpType
ACT = mybir.ActivationFunctionType
AX_X = mybir.AxisListType.X
F32 = mybir.dt.float32
F32R = mybir.dt.float32r
I32 = mybir.dt.int32

P = 128
D = 512
KC = D // P
NB = 8
BT = 128
TOK = NB * BT
H = TOK // 2
HB = NB // 2
E = 8
R = 16
R1 = 64
NCB = 8
F = 1376
NJ = -(-F // P)
FP = NJ * P
AW = E * R + E
G4 = 4
STACKED = 2 * G4 * R
UP_PARTS = 16 * 12

GATE, UP, TDOWN, SPARE, DOWN = 0, 1, 2, 3, 4


def program(nc, t):
    with ExitStack() as ctx:
        cursor = [-(-nc.sbuf_base // 64) * 64]

        def sb(name, shape, dt=F32, at=None):
            n = 4
            for s in shape[1:]:
                n *= s
            off = cursor[0] if at is None else at
            if at is None:
                cursor[0] += -(-n // 64) * 64
            return nc.alloc_sbuf_tensor_at(name, list(shape), dt, offset=off)

        def sem(name):
            return ctx.enter_context(nc.semaphore(name))

        ps = ctx.enter_context(nc.psum_tensor("ps", [P, 8, 512], F32))

        y = sb("y", [P, KC, TOK])
        y_hi = sb("y_hi", [P, KC, TOK], F32R)
        y_lo = sb("y_lo", [P, KC, TOK], F32R)

        aw = sb("aw", [P, KC, AW])
        consts = sb("consts", [P, P + 2 * H + 2 * E + 2])
        ident = consts[:, 0:P]
        up_mask = consts[:, P:P + H]
        pair_mask = consts[:, P + H:P + 2 * H]
        e_iota = consts[:, P + 2 * H:P + 2 * H + E]
        e_rank = consts[:, P + 2 * H + E:P + 2 * H + 2 * E]
        minus_b_lo = consts[:, P + 2 * H + 2 * E:P + 2 * H + 2 * E + 1]
        minus_t_lo = consts[:, P + 2 * H + 2 * E + 1:P + 2 * H + 2 * E + 2]
        lang_i = sb("lang_i", [P, NB], I32)
        lang_f = sb("lang_f", [P, NB])
        bias = sb("bias", [P, NB, E])
        rt = sb("rt", [P, 12, HB, E])
        rs1 = sb("rs1", [P, 10, HB])
        gates = sb("gates", [P, HB, E])
        gated = sb("gated", [P, HB, E, R])
        gated1 = sb("gated1", [P, HB, E, R])
        gh_hi = sb("gh_hi", [P, TOK], F32R)
        gh_lo = sb("gh_lo", [P, TOK], F32R)
        early = cursor[0]
        lb1 = sb("lb1", [R1, D])
        la1 = sb("la1", [R1, D])
        b0 = sb("b0", [P, D])
        b0_hi = sb("b0_hi", [P, D], F32R)
        b0_lo = sb("b0_lo", [P, D], F32R)
        slog = sb("slog", [P, KC * KC])
        scale = sb("scale", [P, KC * KC])
        rscale = sb("rscale", [P, KC * KC])
        cbk = sb("cbk", [P, NCB])
        cbt = sb("cbt", [P, 6, NCB])

        region = cursor[0]
        w0 = sb("w0", [P, KC, D])
        w0_hi = sb("w0_hi", [P, KC, D], F32R)
        w0_lo = sb("w0_lo", [P, KC, D], F32R)
        w1q = sb("w1q", [P, KC, D])
        region2 = cursor[0]
        w1 = sb("w1", [P, KC, D])
        delta = sb("delta", [P, KC, D])
        w1n = sb("w1n", [P, KC, D])
        region_end = cursor[0]
        w1t_hi = sb("w1t_hi", [P, KC, D], F32R, at=region2 + 2 * KC * D * 4)
        w1t_lo = sb("w1t_lo", [P, KC, D], F32R)

        KB = 1024
        wgu_hi = sb("wgu_hi", [P, 2, 2, KC, P], F32R, at=region)
        wgu_lo = sb("wgu_lo", [P, 2, 2, KC, P], F32R, at=region + 8 * KB)
        wd_hi = sb("wd_hi", [P, 2, D], F32R, at=region + 16 * KB)
        wd_lo = sb("wd_lo", [P, 2, D], F32R, at=region + 20 * KB)
        bl = sb("bl", [P, 2, 2, 2, P], F32R, at=region + 24 * KB)
        ad = sb("ad", [P, 2, HB, G4, R], F32R, at=region + 28 * KB)
        act_hi = sb("act_hi", [P, 2, H], F32R, at=region2 + 16 * KB)
        act_lo = sb("act_lo", [P, 2, H], F32R, at=region2 + 20 * KB)
        act = sb("act", [P, 2, H], at=region2 + 24 * KB)
        silu_g = sb("silu_g", [P, 2, H], at=region2 + 28 * KB)
        tg = sb("tg", [P, 2, H], F32R, at=region2)
        tu = sb("tu", [P, 2, H], F32R, at=region2 + 4 * KB)
        td = sb("td", [P, H], F32R, at=region2 + 8 * KB)
        tm = sb("tm", [P, H], at=region2 + 10 * KB)
        t_hi = sb("t_hi", [P, H], F32R, at=region2 + 12 * KB)
        t_lo = sb("t_lo", [P, H], F32R, at=region2 + 14 * KB)

        wgu = sb("wgu", [P, 2, 2, KC, P])
        wd = sb("wd", [P, 2, D])
        blr = sb("blr", [P, 2, 2, 2, P])
        agr = sb("agr", [P, NB, KC, 2, R])
        ag = sb("ag", [P, 4, KC, 2, 2, 2, R], F32R)
        adr = sb("adr", [P, NB, NJ, R])
        bdr = sb("bdr", [P, 2, D])
        bd = sb("bd", [P, 4, D], F32R)
        a3r = sb("a3r", [P, 2, D])
        a3 = sb("a3", [P, 4, D], F32R)
        b3r = sb("b3r", [P, NB, KC, R])
        b_part = sb("b_part", [P, D])
        b3 = sb("b3", [P, KC, NB, G4, R], F32R, at=early)
        idx = sb("idx", [1, 2 * NB], I32)
        assert cursor[0] <= nc.sbuf_usable_end

        ld_aw, ld_l1, ld_c, ld_small, ld_w1, ld_w0, ld_b0, ld_idx = (
            sem(n) for n in ("ld_aw", "ld_l1", "ld_c", "ld_small", "ld_w1", "ld_w0", "ld_b0", "ld_idx"))
        ld_x = [sem("ld_x0"), sem("ld_x1")]
        ld_ag, ld_ad, ld_b3 = sem("ld_ag"), sem("ld_ad"), sem("ld_b3")
        ld_bd, ld_a3 = sem("ld_bd"), sem("ld_a3")
        ld_wgu = [sem("ld_wgu0"), sem("ld_wgu1")]
        ld_wd = [sem("ld_wd0"), sem("ld_wd1")]
        ld_bl = [sem("ld_bl0"), sem("ld_bl1")]
        ld_t, st_out = sem("ld_t"), sem("st_out")
        s_delta, s_hlog, s_l0, s_ght, s_w1t, s_l1 = (
            sem(n) for n in ("s_delta", "s_hlog", "s_l0", "s_ght", "s_w1t", "s_l1"))
        s_ta, s_g, s_u, s_d, s_td, s_dn, s_t3, s_o3 = (
            sem(n) for n in ("s_ta", "s_g", "s_u", "s_d", "s_td", "s_dn", "s_t3", "s_o3"))
        a_dc, a_es, a_exp, a_yh, a_w0, a_b0, a_gh, a_w1t = (
            sem(n) for n in ("a_dc", "a_es", "a_exp", "a_yh", "a_w0", "a_b0", "a_gh", "a_w1t"))
        a_th, a_silu, a_ah, a_wg, a_wd, a_bl = (sem(n) for n in ("a_th", "a_silu", "a_ah", "a_wg", "a_wd", "a_bl"))
        v_chain, v_rs, v_cb, v_dm, v_gate, v_y, v_yl, v_w0, v_b0, v_gh, v_q, v_w1t = (
            sem(n) for n in ("v_chain", "v_rs", "v_cb", "v_dm", "v_gate", "v_y", "v_yl", "v_w0", "v_b0",
                             "v_gh", "v_q", "v_w1t"))
        v_tm, v_tl, v_act, v_al, v_wg, v_wd, v_ad, v_bl, v_out = (
            sem(n) for n in ("v_tm", "v_tl", "v_act", "v_al", "v_wg", "v_wd", "v_ad", "v_bl", "v_out"))
        p_chain, p_n, p_w, p_ag, p_ad, p_bd, p_a3, p_b3 = (
            sem(n) for n in ("p_chain", "p_n", "p_w", "p_ag", "p_ad", "p_bd", "p_a3", "p_b3"))

        def half(h):
            return slice(h * H, (h + 1) * H)

        def ad_raw(j, h):
            return adr[:, HB * h:HB * (h + 1), bass.ds(j, 1), :].rearrange("p b j r -> p b (j r)")

        block = ctx.enter_context(nc.Block())

        @block.sync
        def _(sp):
            def chunks(ap):
                return ap.rearrange("(c p) n -> p c n", p=P)

            sp.dma_start(aw[:], chunks(t["aw"])).then_inc(ld_aw, 16)
            sp.dma_start(lb1[:], t["lb1"]).then_inc(ld_l1, 16)
            sp.dma_start(la1[:], t["la1"]).then_inc(ld_l1, 16)
            xv = chunks(t["x"])
            for c in range(0, KC, 2):
                sp.dma_start(y[:, c:c + 2, half(0)], xv[:, c:c + 2, half(0)]).then_inc(ld_x[0], 16)
            sp.dma_start(consts[:], t["consts"]).then_inc(ld_c, 16)
            sp.dma_start(lang_i[:], t["lang"].partition_broadcast(P)).then_inc(ld_small, 16)
            sp.dma_start(cbk[:], t["cb"].partition_broadcast(P)).then_inc(ld_small, 16)
            sp.dma_start(slog[:].rearrange("p (c g) -> p c g", g=KC), chunks(t["slog"])).then_inc(ld_small, 16)
            w1v, w0v = chunks(t["w1"]), chunks(t["w0"])
            for c in range(0, KC, 2):
                sp.dma_start(w1[:, c:c + 2], w1v[:, c:c + 2]).then_inc(ld_w1, 16)
            for c in range(0, KC, 2):
                sp.dma_start(w0[:, c:c + 2], w0v[:, c:c + 2]).then_inc(ld_w0, 16)
            for c in range(0, KC, 2):
                sp.dma_start(y[:, c:c + 2, half(1)], xv[:, c:c + 2, half(1)]).then_inc(ld_x[1], 16)
            sp.dma_start(b0[:], t["b0"]).then_inc(ld_b0, 16)
            sp.dma_start(idx[:, 0:NB], t["idx2"]).then_inc(ld_idx, 16)
            sp.dma_start(idx[:, NB:2 * NB], t["idx3"]).then_inc(ld_idx, 16)
            sp.wait_ge(ld_idx, 32)

            def adapter2(b):
                return sp.value_load(idx[0:1, b:b + 1], min_val=0, max_val=15)

            def adapter3(b):
                return sp.value_load(idx[0:1, NB + b:NB + b + 1], min_val=0, max_val=7)

            def grouped(tile_ap, b2):
                return tile_ap[b2 * G4 * R:(b2 + 1) * G4 * R]

            def repeated(ap):
                r, n = ap.shape
                return ap.unsqueeze(0).to_broadcast([G4, r, n])

            def load_a(b):
                i2 = adapter2(b)
                sp.dma_start(agr[:, b], t["agu"][bass.ds(i2, 1)].rearrange("a p n -> (a p) n")).then_inc(ld_ag, 16)
                sp.dma_start(adr[:, b], t["ad"][bass.ds(i2, 1)].rearrange("a p n -> (a p) n")).then_inc(ld_ad, 16)

            def load_b3(b):
                i3 = adapter3(b)
                sp.dma_start(b3r[:, b], t["b3"][bass.ds(i3, 1)].rearrange("a p n -> (a p) n")).then_inc(ld_b3, 16)

            def load_bd_a3(h):
                if h == 1:
                    sp.wait_ge(p_bd, 1)
                    sp.wait_ge(p_a3, 1)
                for b in range(HB):
                    i2 = adapter2(HB * h + b)
                    i3 = adapter3(HB * h + b)
                    sp.dma_start(grouped(bdr[:, b // 2], b % 2),
                                 repeated(t["bd"][bass.ds(i2, 1)].rearrange("a r n -> (a r) n"))).then_inc(ld_bd, 16)
                    sp.dma_start(grouped(a3r[:, b // 2], b % 2),
                                 repeated(t["a3"][bass.ds(i3, 1)].rearrange("a r n -> (a r) n"))).then_inc(ld_a3, 16)

            def load_wgu(j, q, s, h):
                if not (isinstance(q, int) and q == 0):
                    sp.wait_ge(a_wg, 2 * q + s - 1)
                    sp.wait_ge(v_wg, 2 * q + s - 1)
                    sp.wait_ge(v_bl, 2 * q + s - 1)
                sp.dma_start(wgu[:, s], t["wgu"][bass.ds(j, 1)].rearrange("j p n -> (j p) n")).then_inc(ld_wgu[s], 16)
                for b in range(HB):
                    src = t["bgu"][bass.ds(bl_idx[HB * h + b], 1), bass.ds(j, 1)].rearrange("a j r n -> (a j r) n")
                    sp.dma_start(grouped(blr[:, s, b // 2].rearrange("p u f -> p (u f)"), b % 2),
                                 repeated(src)).then_inc(ld_bl[s], 16)

            def load_wd(j, q, s):
                if not (isinstance(q, int) and q == 0):
                    sp.wait_ge(a_wd, 2 * q + s - 1)
                    sp.wait_ge(v_wd, 2 * q + s - 1)
                sp.dma_start(wd[:, s], t["wd"][bass.ds(j, 1)].rearrange("j p n -> (j p) n")).then_inc(ld_wd[s], 16)

            for b in range(NB):
                load_a(b)
            bl_idx = {b: adapter2(b) for b in range(HB)}
            load_wgu(0, 0, 0, 0)
            load_wgu(1, 0, 1, 0)
            for b in range(NB):
                load_b3(b)
            load_bd_a3(0)
            for h in range(2):
                n0 = NJ * h
                for j in (0,):
                    load_wd(j, (n0 + j) // 2, (n0 + j) % 2)
                    load_wgu(j + 2, (n0 + j + 2) // 2, (n0 + j) % 2, h)
                with sp.Fori(0, 4) as i:
                    for k in range(2):
                        n = n0 + 1 + k
                        load_wd(1 + k + 2 * i, n // 2 + i, n % 2)
                        load_wgu(3 + k + 2 * i, (n + 2) // 2 + i, n % 2, h)
                if h == 0:
                    bl_idx.update({b: adapter2(b) for b in range(HB, NB)})
                    load_bd_a3(1)
                for j in (9, 10):
                    n = n0 + j
                    load_wd(j, n // 2, n % 2)
                    if h == 0:
                        load_wgu(j - 9, (n + 2) // 2, n % 2, 1)
            ov = t["out"].rearrange("(c p) n -> p c n", p=P)
            for h in range(2):
                for c in range(KC):
                    sp.wait_ge(v_out, KC * h + c + 1)
                    sp.dma_start(ov[:, c, half(h)], y[:, c, half(h)]).then_inc(st_out, 16)
            sp.wait_ge(st_out, 16 * 2 * KC)

        @block.tensor
        def _(pe):
            def three(out, w_hi, w_lo, r_hi, r_lo, start, stop):
                nc.tensor.matmul(out, w_hi, r_hi, start=start, stop=False, skip_group_check=True)
                nc.tensor.matmul(out, w_hi, r_lo, start=False, stop=False, skip_group_check=True)
                return nc.tensor.matmul(out, w_lo, r_hi, start=False, stop=stop, skip_group_check=True)

            def y_ready(group):
                pe.wait_ge(a_yh, KC * (group + 1))
                pe.wait_ge(v_yl, KC * (group + 1))

            pe.wait_ge(ld_l1, 32)
            for o in range(KC):
                nc.tensor.matmul(ps[:, o], lb1[:, o * P:(o + 1) * P], la1[:], start=True, stop=True).then_inc(s_delta, 1)

            pe.wait_ge(ld_aw, 16)
            for b in range(NB):
                if b % HB == 0:
                    pe.wait_ge(ld_x[b // HB], 32)
                out = ps[:, 4 + b // 2, (b % 2) * AW:(b % 2 + 1) * AW]
                for c in range(KC):
                    last = nc.tensor.matmul(out, y[:, c, b * BT:(b + 1) * BT], aw[:, c],
                                            start=(c == 0), stop=(c == KC - 1))
                if b % 2:
                    last.then_inc(s_hlog, 1)

            def l0_base(h, o):
                for c in range(KC):
                    three(ps[:, 4 * h + o], w0_hi[:, c, o * P:(o + 1) * P], w0_lo[:, c, o * P:(o + 1) * P],
                          y_hi[:, c, half(h)], y_lo[:, c, half(h)], c == 0, False)

            def l0_lora(h):
                pe.wait_ge(a_b0, 1)
                pe.wait_ge(v_b0, 1)
                pe.wait_ge(a_gh, h + 1)
                pe.wait_ge(v_gh, h + 1)
                for o in range(KC):
                    three(ps[:, 4 * h + o], b0_hi[:, o * P:(o + 1) * P], b0_lo[:, o * P:(o + 1) * P],
                          gh_hi[:, half(h)], gh_lo[:, half(h)], False, True).then_inc(s_l0, 1)

            y_ready(0)
            pe.wait_ge(a_w0, KC)
            pe.wait_ge(v_w0, KC)
            pe.wait_ge(a_dc, KC)
            for o in range(3):
                l0_base(0, o)
            pe.wait_ge(ld_c, 16)
            for h in range(2):
                pe.wait_ge(v_gate, h + 1)
                for b in range(HB):
                    last = nc.tensor.transpose(ps[:, 4 + h, b * BT:(b + 1) * BT],
                                               (gated if h == 0 else gated1)[:, b].rearrange("p e r -> p (e r)"), ident)
                last.then_inc(s_ght, 1)
            l0_base(0, 3)
            l0_lora(0)
            y_ready(1)
            pe.wait_ge(a_gh, 2)
            pe.wait_ge(v_gh, 2)
            for o in range(3):
                l0_base(1, o)
            pe.wait_ge(v_y, KC)
            for o in range(KC):
                pe.wait_ge(p_w, o + 1)
            for c in range(KC):
                for o in range(KC):
                    last = nc.tensor.transpose(ps[:, c, o * P:(o + 1) * P], w1q[:, o, c * P:(c + 1) * P], ident)
                last.then_inc(s_w1t, 1)
            l0_base(1, 3)
            l0_lora(1)

            def l1(h, o):
                for c in range(KC):
                    last = three(ps[:, 4 * h + o], w1t_hi[:, c, o * P:(o + 1) * P], w1t_lo[:, c, o * P:(o + 1) * P],
                                 y_hi[:, c, half(h)], y_lo[:, c, half(h)], c == 0, c == KC - 1)
                last.then_inc(s_l1, 1)

            def t_up(h):
                y_ready(4 + h)
                pe.wait_ge(p_ag, h + 1)
                for p in range(2):
                    out = ps[:, SPARE, p * 2 * BT:(p + 1) * 2 * BT]
                    cols = slice(h * H + p * 2 * BT, h * H + (p + 1) * 2 * BT)
                    for c in range(KC):
                        w = ag[:, 2 * h + p, c].rearrange("p u b s r -> p (u b s r)")
                        nc.tensor.matmul(out, w, y_hi[:, c, cols], start=(c == 0), stop=False, skip_group_check=True)
                        last = nc.tensor.matmul(out, w, y_lo[:, c, cols], start=False, stop=(c == KC - 1), skip_group_check=True)
                last.then_inc(s_ta, 1)

            pe.wait_ge(a_w1t, KC)
            pe.wait_ge(v_w1t, KC)
            y_ready(2)
            for o in range(KC):
                l1(0, o)
            y_ready(3)
            l1(1, 0)
            l1(1, 1)
            t_up(0)
            l1(1, 2)
            l1(1, 3)

            def gate_or_up(which, bank, s, h, done):
                for c in range(KC):
                    three(ps[:, bank], wgu_hi[:, s, which, c], wgu_lo[:, s, which, c],
                          y_hi[:, c, half(h)], y_lo[:, c, half(h)], c == 0, False)
                tt = tg if which == 0 else tu
                for p in range(2):
                    last = nc.tensor.matmul(ps[:, bank, p * 2 * BT:(p + 1) * 2 * BT], bl[:, s, p, which],
                                            tt[:, h, p * 2 * BT:(p + 1) * 2 * BT], start=False, stop=(p == 1),
                                            skip_group_check=True)
                last.then_inc(done, 1)

            def gate(q, s, h, first=False):
                n = 2 * q + s
                pe.wait_ge(a_wg, n + 1)
                pe.wait_ge(v_wg, n + 1)
                pe.wait_ge(v_bl, n + 1)
                pe.wait_ge(ld_t, UP_PARTS * (h + 1))
                if not first:
                    pe.wait_ge(a_silu, n)
                gate_or_up(0, GATE, s, h, s_g)

            def up(q, s, h, first=False):
                if not first:
                    pe.wait_ge(v_act, 2 * q + s)
                gate_or_up(1, UP, s, h, s_u)

            def t_down(q, s, first):
                n = 2 * q + s
                pe.wait_ge(a_ah, n + 1)
                pe.wait_ge(v_al, n + 1)
                pe.wait_ge(p_ad, n + 1)
                pe.wait_ge(v_ad, n + 1)
                for p in range(2):
                    cols = slice(p * 2 * BT, (p + 1) * 2 * BT)
                    out = ps[:, TDOWN, cols]
                    w = ad[:, s, 2 * p:2 * p + 2].rearrange("p b g r -> p (b g r)")
                    nc.tensor.matmul(out, w, act_hi[:, s, cols], start=(first and p == 0), stop=False,
                                     skip_group_check=True)
                    last = nc.tensor.matmul(out, w, act_lo[:, s, cols], start=False, stop=False,
                                            skip_group_check=True)
                return last

            def down(q, s, first=False):
                n = 2 * q + s
                pe.wait_ge(a_wd, n + 1)
                pe.wait_ge(v_wd, n + 1)
                for o in range(KC):
                    last = three(ps[:, DOWN + o], wd_hi[:, s, o * P:(o + 1) * P], wd_lo[:, s, o * P:(o + 1) * P],
                                 act_hi[:, s], act_lo[:, s], first, False)
                last.then_inc(s_d, 1)

            def down_lora(h):
                pe.wait_ge(p_bd, h + 1)
                pe.wait_ge(v_tl, 3 + 2 * h)
                for o in range(KC):
                    for p in range(2):
                        cols = slice(p * 2 * BT, (p + 1) * 2 * BT)
                        last = nc.tensor.matmul(ps[:, DOWN + o, cols], bd[:, 2 * h + p, o * P:(o + 1) * P], td[:, cols],
                                                start=False, stop=(p == 1), skip_group_check=True)
                    last.then_inc(s_dn, 1)

            def t_three(h):
                y_ready(6 + h)
                pe.wait_ge(p_b3, h + 1)
                for p in range(2):
                    out = ps[:, SPARE, p * 2 * BT:(p + 1) * 2 * BT]
                    cols = slice(h * H + p * 2 * BT, h * H + (p + 1) * 2 * BT)
                    for c in range(KC):
                        w = b3[:, c, HB * h + 2 * p:HB * h + 2 * p + 2].rearrange("p b g r -> p (b g r)")
                        nc.tensor.matmul(out, w, y_hi[:, c, cols], start=(c == 0), stop=False, skip_group_check=True)
                        last = nc.tensor.matmul(out, w, y_lo[:, c, cols], start=False, stop=(c == KC - 1), skip_group_check=True)
                last.then_inc(s_t3, 1)

            def out_three(h, o, bank):
                if h == 0 and o > 0:
                    pe.wait_ge(v_out, o)
                pe.wait_ge(p_a3, h + 1)
                pe.wait_ge(v_tl, 4 + 2 * h)
                for p in range(2):
                    cols = slice(p * 2 * BT, (p + 1) * 2 * BT)
                    last = nc.tensor.matmul(ps[:, bank, cols], a3[:, 2 * h + p, o * P:(o + 1) * P], td[:, cols],
                                            start=(p == 0), stop=True, skip_group_check=True)
                last.then_inc(s_o3, 1)

            for h in range(2):
                n0 = NJ * h

                def at(j):
                    return (n0 + j) // 2, (n0 + j) % 2

                y_ready(4 + h)
                gate(*at(0), h, first=(h == 0))
                if h == 1:
                    down_lora(0)
                up(*at(0), h, first=(h == 0))
                if h == 0:
                    pe.wait_ge(v_tm, 1)
                    t_up(1)
                gate(*at(1), h)
                if h == 1:
                    t_three(0)
                up(*at(1), h)
                pe.wait_ge(v_y, KC * (4 if h == 0 else 5))
                if h == 1:
                    pe.wait_ge(v_tm, 3)
                t_down(*at(0), True)
                down(*at(0), first=True)
                gate(*at(2), h)
                if h == 1:
                    pe.wait_ge(v_tm, 4)
                    out_three(0, 0, SPARE)
                up(*at(2), h)
                if h == 1:
                    out_three(0, 1, SPARE)
                t_down(*at(1), False)
                down(*at(1))
                if h == 1:
                    out_three(0, 2, SPARE)
                with pe.Fori(0, 4) as i:
                    for k in range(2):
                        q, s = at(3 + k)
                        gate(q + i, s, h)
                        up(q + i, s, h)
                        q, s = at(2 + k)
                        t_down(q + i, s, False)
                        down(q + i, s)
                if h == 1:
                    out_three(0, 3, SPARE)
                t_down(*at(NJ - 1), False).then_inc(s_td, 1)
                down(*at(NJ - 1))
            down_lora(1)
            pe.wait_ge(v_out, KC)
            t_three(1)
            pe.wait_ge(v_tm, 6)
            for o in range(KC):
                out_three(1, o, (GATE, UP, TDOWN, SPARE)[o])

        @block.scalar
        def _(act_e):
            def cast(out, in_):
                return nc.scalar.activation(out, in_, ACT.Copy)

            def split_y(h, c):
                return cast(y_hi[:, c, half(h)], y[:, c, half(h)]).then_inc(a_yh, 1)

            def result_hi(layer, h):
                if layer < 2:
                    act_e.wait_ge((s_l0, s_l1)[layer], KC * (h + 1))
                for c in range(KC):
                    act_e.wait_ge(v_y, KC * (2 * layer + h) + c + 1)
                    split_y(h, c)

            for o in range(KC):
                act_e.wait_ge(s_delta, o + 1)
                nc.scalar.activation(delta[:, o], ps[:, o], ACT.Copy, scale=0.5).then_inc(a_dc, 1)
            act_e.wait_ge(ld_small, 48)
            nc.scalar.activation(scale[:], slog[:], ACT.Exp).then_inc(a_es, 1)
            act_e.wait_ge(ld_x[0], 32)
            for c in range(KC):
                split_y(0, c)
            act_e.wait_ge(ld_w0, 32)
            for c in range(KC):
                cast(w0_hi[:, c], w0[:, c]).then_inc(a_w0, 1)
            act_e.wait_ge(ld_b0, 16)
            cast(b0_hi[:], b0[:]).then_inc(a_b0, 1)
            act_e.wait_ge(ld_x[1], 32)
            for h in range(2):
                act_e.wait_ge(v_dm, h + 1)
                nc.scalar.activation(rs1[:, 4 + h], rs1[:, 2 + h], ACT.Exp).then_inc(a_exp, 1)
                if h == 0:
                    for c in range(KC):
                        split_y(1, c)
            for h in range(2):
                act_e.wait_ge(s_ght, h + 1)
                cast(gh_hi[:, half(h)], ps[:, 4 + h]).then_inc(a_gh, 1)
            result_hi(0, 0)
            for c in range(KC):
                act_e.wait_ge(s_w1t, c + 1)
                cast(w1t_hi[:, c], ps[:, c]).then_inc(a_w1t, 1)
            result_hi(0, 1)

            def split_wgu(q, s):
                n = 2 * q + s
                if not (isinstance(q, int) and q == 0):
                    act_e.wait_ge(s_u, n - 1)
                act_e.wait_ge(ld_wgu[s], 16 * (q + 1))
                cast(wgu_hi[:, s].rearrange("p u c f -> p (u c f)"),
                     wgu[:, s].rearrange("p u c f -> p (u c f)")).then_inc(a_wg, 1)
                act_e.wait_ge(ld_bl[s], 16 * HB * (q + 1))
                cast(bl[:, s].rearrange("p a u f -> p (a u f)"),
                     blr[:, s].rearrange("p a u f -> p (a u f)")).then_inc(a_bl, 1)

            def split_wd(q, s):
                n = 2 * q + s
                if not (isinstance(q, int) and q == 0):
                    act_e.wait_ge(s_d, n - 1)
                act_e.wait_ge(ld_wd[s], 16 * (q + 1))
                cast(wd_hi[:, s], wd[:, s]).then_inc(a_wd, 1)

            act_e.wait_ge(s_l0, 2 * KC)
            split_wgu(0, 0)
            split_wgu(0, 1)
            result_hi(1, 0)

            def silu(q, s):
                n = 2 * q + s
                act_e.wait_ge(s_g, n + 1)
                if not (isinstance(q, int) and q == 0):
                    act_e.wait_ge(v_act, n - 1)
                nc.scalar.activation(silu_g[:, s], ps[:, GATE], ACT.Silu).then_inc(a_silu, 1)

            def act_split(q, s):
                n = 2 * q + s
                act_e.wait_ge(v_act, n + 1)
                if not (isinstance(q, int) and q == 0):
                    act_e.wait_ge(s_d, n - 1)
                cast(act_hi[:, s], act[:, s]).then_inc(a_ah, 1)

            def ranks_hi(k):
                act_e.wait_ge(v_tm, k)
                cast(t_hi[:], tm[:]).then_inc(a_th, 1)

            def stack_up(h):
                act_e.wait_ge(a_th, h + 1)
                act_e.wait_ge(v_tl, h + 1)
                for u, dst in enumerate((tg, tu)):
                    for b in range(2):
                        to, row = b * G4 * R, (u * 2 + b) * 2 * R
                        for src, rows, at_ in ((t_hi, 2 * R, 0), (t_hi, R, 2 * R), (t_lo, R, 3 * R)):
                            act_e.dma_start(dst[to + at_:to + at_ + rows, h].bitcast(F32),
                                            src[row:row + rows].bitcast(F32)).then_inc(ld_t, 16)

            ranks_hi(1)
            stack_up(0)
            result_hi(1, 1)
            for h in range(2):
                n0 = NJ * h

                def at(j):
                    return (n0 + j) // 2, (n0 + j) % 2

                silu(*at(0))
                if h == 1:
                    result_hi(2, 0)
                split_wd(*at(0))
                act_split(*at(0))
                if h == 0:
                    act_e.wait_ge(ld_t, UP_PARTS)
                    ranks_hi(2)
                    stack_up(1)
                split_wgu(*at(2))
                split_wd(*at(1))
                silu(*at(1))
                if h == 1:
                    ranks_hi(4)
                act_split(*at(1))
                split_wgu(*at(3))
                silu(*at(2))
                split_wd(*at(2))
                act_split(*at(2))
                split_wgu(*at(4))
                with act_e.Fori(0, 3) as i:
                    for k in range(2):
                        q, s = at(3 + k)
                        split_wd(q + i, s)
                        silu(q + i, s)
                        act_split(q + i, s)
                        split_wgu(q + i + 1, s)
                for j in (9, 10):
                    split_wd(*at(j))
                    silu(*at(j))
                    act_split(*at(j))
                    if h == 0:
                        split_wgu(*at(j + 2))
                if h == 0:
                    act_e.wait_ge(ld_t, 2 * UP_PARTS)
                ranks_hi(3 + 2 * h)
            result_hi(2, 1)
            ranks_hi(6)

        @block.vector
        def _(dve):
            count = [0]

            def link(ins):
                count[0] += 1
                ins.then_inc(v_chain, 1)
                dve.wait_ge(v_chain, count[0])

            TT, TS = nc.vector.tensor_tensor, nc.vector.tensor_scalar

            def lo_of(out, whole, hi):
                return TT(out, whole, hi.bitcast(F32), ALU.subtract)

            def y_lo_of(group, h, c):
                dve.wait_ge(a_yh, KC * group + c + 1)
                lo_of(y_lo[:, c, half(h)], y[:, c, half(h)], y_hi[:, c, half(h)]).then_inc(v_yl, 1)

            dve.wait_ge(ld_small, 48)
            c_abs, c_n, thr, u, step = (cbt[:, k] for k in range(5))
            link(TS(c_abs, cbk[:], -1.0, None, ALU.mult))
            link(TT(c_abs, c_abs, cbk[:], ALU.max))
            link(nc.vector.tensor_reduce(cbt[:, 5, 0:1], c_abs, AX_X, ALU.max))
            link(TS(cbt[:, 5, 0:1], cbt[:, 5, 0:1], 1e-8, None, ALU.max))
            link(nc.vector.reciprocal(cbt[:, 5, 1:2], cbt[:, 5, 0:1]))
            link(TS(c_n, cbk[:], cbt[:, 5, 1:2], None, ALU.mult))
            TT(step[:, 0:7], c_n[:, 1:8], c_n[:, 0:7], ALU.subtract)
            link(TT(thr[:, 0:7], c_n[:, 1:8], c_n[:, 0:7], ALU.add))
            link(TS(thr[:, 0:7], thr[:, 0:7], 0.5, None, ALU.mult))
            link(nc.vector.tensor_copy(u[:, 3:4], thr[:, 3:4]))
            TT(u[:, 1:2], thr[:, 1:2], thr[:, 3:4], ALU.min)
            link(TT(u[:, 5:6], thr[:, 5:6], thr[:, 3:4], ALU.max))
            TT(u[:, 0:1], thr[:, 0:1], u[:, 1:2], ALU.min)
            TT(u[:, 6:7], thr[:, 6:7], u[:, 5:6], ALU.max)
            TT(c_abs[:, 2:3], thr[:, 2:3], u[:, 1:2], ALU.max)
            link(TT(c_abs[:, 4:5], thr[:, 4:5], u[:, 3:4], ALU.max))
            TT(u[:, 2:3], c_abs[:, 2:3], u[:, 3:4], ALU.min)
            link(TT(u[:, 4:5], c_abs[:, 4:5], u[:, 5:6], ALU.min))
            dve.wait_ge(a_es, 1)
            nc.vector.reciprocal(rscale[:], scale[:]).then_inc(v_rs, 1)
            link(nc.vector.tensor_copy(lang_f[:], lang_i[:]))
            dve.wait_ge(ld_c, 16)
            link(TT(bias[:], lang_f[:].unsqueeze(2).to_broadcast([P, NB, E]),
                    e_iota.unsqueeze(1).to_broadcast([P, NB, E]), ALU.is_equal))

            for c in range(KC):
                y_lo_of(0, 0, c)
            for c in range(KC):
                dve.wait_ge(a_w0, c + 1)
                lo_of(w0_lo[:, c], w0[:, c], w0_hi[:, c]).then_inc(v_w0, 1)
            dve.wait_ge(a_b0, 1)
            lo_of(b0_lo[:], b0[:], b0_hi[:]).then_inc(v_b0, 1)

            def router_top2(h):
                hl = ps[:, 4 + 2 * h:6 + 2 * h, 0:2 * AW].rearrange("p k (b n) -> p k b n", b=2)
                dve.wait_ge(s_hlog, 2 * h + 2)
                lg, eq, sc, oh1, lg2, oh2 = (rt[:, 6 * h + k] for k in range(6))
                m1, m2 = rs1[:, 0], rs1[:, 1]
                rank = e_rank.unsqueeze(1).to_broadcast([P, HB, E])

                def wide(v):
                    return v.unsqueeze(2).to_broadcast([P, HB, E])

                for k in range(2):
                    last = nc.vector.scalar_tensor_tensor(lg[:, 2 * k:2 * k + 2],
                                                          bias[:, HB * h + 2 * k:HB * h + 2 * k + 2], 5.0,
                                                          hl[:, k, :, E * R:AW], ALU.mult, ALU.add)
                link(last)
                link(nc.vector.tensor_reduce(m1, lg, AX_X, ALU.max))
                for src, m, oh in ((lg, m1, oh1), (lg2, m2, oh2)):
                    if src is lg2:
                        link(nc.vector.scalar_tensor_tensor(lg2, oh1, -3.0e38, lg, ALU.mult, ALU.add))
                        link(nc.vector.tensor_reduce(m2, lg2, AX_X, ALU.max))
                    link(TT(eq, src, wide(m), ALU.is_equal))
                    link(TT(sc, eq, rank, ALU.mult))
                    link(nc.vector.tensor_reduce(rs1[:, 6], sc, AX_X, ALU.max))
                    link(TT(oh, rank, wide(rs1[:, 6]), ALU.is_equal))
                TT(rs1[:, 2 + h], m2, m1, ALU.subtract).then_inc(v_dm, 1)

            def router_gates(h):
                hl = ps[:, 4 + 2 * h:6 + 2 * h, 0:2 * AW].rearrange("p k (b n) -> p k b n", b=2)
                oh1, oh2 = rt[:, 6 * h + 3], rt[:, 6 * h + 5]
                w1_, w2_ = rs1[:, 7], rs1[:, 8]
                dve.wait_ge(a_exp, h + 1)
                link(TS(rs1[:, 6], rs1[:, 4 + h], 1.0, None, ALU.add))
                link(nc.vector.reciprocal(w1_, rs1[:, 6]))
                link(TT(w2_, rs1[:, 4 + h], w1_, ALU.mult))
                link(TT(oh1, oh1, w1_.unsqueeze(2).to_broadcast([P, HB, E]), ALU.mult))
                link(TT(oh2, oh2, w2_.unsqueeze(2).to_broadcast([P, HB, E]), ALU.mult))
                link(TT(oh1, oh1, oh2, ALU.add))
                link(TS(gates[:], oh1, 2.0, None, ALU.mult))
                dst = gated if h == 0 else gated1
                for k in range(2):
                    last = TT(dst[:, 2 * k:2 * k + 2], hl[:, k, :, 0:E * R].rearrange("p b (e r) -> p b e r", e=E),
                              gates[:, 2 * k:2 * k + 2].unsqueeze(3).to_broadcast([P, 2, E, R]), ALU.mult)
                last.then_inc(v_gate, 1)

            router_top2(0)
            router_gates(0)
            for c in range(KC):
                y_lo_of(1, 1, c)
            router_top2(1)
            router_gates(1)

            def quantise(o):
                dve.wait_ge(p_n, o + 1)
                n, q = w1n[:, o], w1q[:, o]
                link(TS(q, n, u[:, 6:7], step[:, 6:7], ALU.is_gt, ALU.mult))
                for k in range(5, -1, -1):
                    link(TS(q, q, step[:, k:k + 1], None, ALU.add))
                    link(nc.vector.scalar_tensor_tensor(q, n, u[:, k:k + 1], q, ALU.is_gt, ALU.mult))
                TS(q, q, c_n[:, 0:1], None, ALU.add).then_inc(v_q, 1)

            def gh_split(h):
                dve.wait_ge(a_gh, h + 1)
                lo_of(gh_lo[:, half(h)], ps[:, 4 + h], gh_hi[:, half(h)]).then_inc(v_gh, 1)

            quantise(0)
            quantise(1)
            gh_split(0)
            gh_split(1)
            quantise(2)
            quantise(3)

            def add_result(done, h, c, bank):
                dve.wait_ge(done, KC * h + c + 1)
                return TT(y[:, c, half(h)], y[:, c, half(h)], ps[:, bank], ALU.add)

            def results(layer, h, done):
                for c in range(KC):
                    add_result(done, h, c, 4 * h + c).then_inc(v_y, 1)
                for c in range(KC):
                    y_lo_of(2 * (layer + 1) + h, h, c)

            results(0, 0, s_l0)
            for c in range(KC):
                dve.wait_ge(a_w1t, c + 1)
                lo_of(w1t_lo[:, c], ps[:, c], w1t_hi[:, c]).then_inc(v_w1t, 1)
            results(0, 1, s_l0)

            def split_wgu(q, s):
                dve.wait_ge(a_wg, 2 * q + s + 1)
                lo_of(wgu_lo[:, s].rearrange("p u c f -> p (u c f)"), wgu[:, s].rearrange("p u c f -> p (u c f)"),
                      wgu_hi[:, s].rearrange("p u c f -> p (u c f)")).then_inc(v_wg, 1)
                dve.wait_ge(a_bl, 2 * q + s + 1)
                whole = bl[:, s].rearrange("p a u f -> p (a u f)")
                nc.vector.scalar_tensor_tensor(whole, whole.bitcast(F32), minus_b_lo,
                                               blr[:, s].rearrange("p a u f -> p (a u f)"),
                                               ALU.mult, ALU.add).then_inc(v_bl, 1)

            def split_wd(q, s):
                dve.wait_ge(a_wd, 2 * q + s + 1)
                lo_of(wd_lo[:, s], wd[:, s], wd_hi[:, s]).then_inc(v_wd, 1)

            def split_ad(q, s, j, h):
                dve.wait_ge(p_ad, 2 * q + s + 1)
                TT(ad[:, s, :, 1], ad_raw(j, h), ad[:, s, :, 0].bitcast(F32), ALU.subtract).then_inc(v_ad, 1)

            def act_up(q, s):
                n = 2 * q + s
                dve.wait_ge(s_u, n + 1)
                dve.wait_ge(a_silu, n + 1)
                if not (isinstance(q, int) and q == 0):
                    dve.wait_ge(a_ah, n - 1)
                    dve.wait_ge(v_al, n - 1)
                TT(act[:, s], silu_g[:, s], ps[:, UP], ALU.mult).then_inc(v_act, 1)

            def act_split(q, s):
                dve.wait_ge(a_ah, 2 * q + s + 1)
                dve.wait_ge(v_act, 2 * q + s + 1)
                lo_of(act_lo[:, s], act[:, s], act_hi[:, s]).then_inc(v_al, 1)

            def ranks_up(h):
                dve.wait_ge(s_ta, h + 1)
                TT(tm[:], ps[:, SPARE], up_mask, ALU.mult).then_inc(v_tm, 1)
                dve.wait_ge(a_th, h + 1)
                lo_of(t_lo[:], tm[:], t_hi[:]).then_inc(v_tl, 1)

            def ranks_stacked(k, done, count_, bank, factor):
                dve.wait_ge(done, count_)
                nc.vector.scalar_tensor_tensor(tm[:], ps[:, bank], factor, pair_mask, ALU.mult, ALU.mult).then_inc(v_tm, 1)
                dve.wait_ge(a_th, k)
                nc.vector.scalar_tensor_tensor(td[:], t_hi[:].bitcast(F32), minus_t_lo, tm[:],
                                               ALU.mult, ALU.add).then_inc(v_tl, 1)

            split_wgu(0, 0)
            split_wgu(0, 1)
            results(1, 0, s_l1)
            add_result(s_l1, 1, 0, 4).then_inc(v_y, 1)
            add_result(s_l1, 1, 1, 5).then_inc(v_y, 1)
            ranks_up(0)
            add_result(s_l1, 1, 2, 6).then_inc(v_y, 1)
            add_result(s_l1, 1, 3, 7).then_inc(v_y, 1)
            for c in range(KC):
                y_lo_of(5, 1, c)

            def out_result(h, c, bank):
                add_result(s_o3, h, c, bank).then_inc(v_out, 1)

            for h in range(2):
                n0 = NJ * h

                def at(j):
                    return (n0 + j) // 2, (n0 + j) % 2

                if h == 1:
                    for c in range(KC):
                        add_result(s_dn, 0, c, DOWN + c).then_inc(v_y, 1)
                    for c in range(KC):
                        y_lo_of(6, 0, c)
                split_wd(*at(0))
                split_ad(*at(0), 0, h)
                act_up(*at(0))
                act_split(*at(0))
                if h == 0:
                    dve.wait_ge(ld_t, UP_PARTS)
                    ranks_up(1)
                split_wgu(*at(2))
                split_wd(*at(1))
                split_ad(*at(1), 1, h)
                if h == 1:
                    ranks_stacked(4, s_t3, 1, SPARE, 2.0)
                act_up(*at(1))
                act_split(*at(1))
                split_wgu(*at(3))
                split_wd(*at(2))
                split_ad(*at(2), 2, h)
                if h == 1:
                    out_result(0, 0, SPARE)
                act_up(*at(2))
                if h == 1:
                    out_result(0, 1, SPARE)
                act_split(*at(2))
                if h == 1:
                    out_result(0, 2, SPARE)
                split_wgu(*at(4))
                with dve.Fori(0, 3) as i:
                    for k in range(2):
                        q, s = at(3 + k)
                        split_wd(q + i, s)
                        split_ad(q + i, s, 3 + k + 2 * i, h)
                        act_up(q + i, s)
                        act_split(q + i, s)
                        split_wgu(q + i + 1, s)
                for j in (9, 10):
                    split_wd(*at(j))
                    split_ad(*at(j), j, h)
                    act_up(*at(j))
                    act_split(*at(j))
                    if h == 0:
                        split_wgu(*at(j + 2))
                if h == 1:
                    out_result(0, 3, SPARE)
                ranks_stacked(3 + 2 * h, s_td, h + 1, TDOWN, 1.0)
            for c in range(KC):
                add_result(s_dn, 1, c, DOWN + c).then_inc(v_y, 1)
            for c in range(KC):
                y_lo_of(7, 1, c)
            ranks_stacked(6, s_t3, 2, SPARE, 2.0)
            for c in range(KC):
                out_result(1, c, (GATE, UP, TDOWN, SPARE)[c])

        @block.gpsimd
        def _(pool):
            count = [0]

            def link(ins):
                count[0] += 1
                ins.then_inc(p_chain, 1)
                pool.wait_ge(p_chain, count[0])

            TT, copy = nc.gpsimd.tensor_tensor, nc.gpsimd.tensor_copy

            def by_group(v, o):
                return v[:, KC * o:KC * (o + 1)].unsqueeze(2).to_broadcast([P, KC, P])

            def groups(v):
                return v.rearrange("p (g n) -> p g n", g=KC)

            pool.wait_ge(ld_w1, 32)
            for o in range(KC):
                pool.wait_ge(a_dc, o + 1)
                link(TT(w1n[:, o], w1[:, o], delta[:, o], ALU.add))
                if o == 0:
                    pool.wait_ge(v_rs, 1)
                TT(groups(w1n[:, o]), groups(w1n[:, o]), by_group(rscale, o), ALU.mult).then_inc(p_n, 1)
            pool.wait_ge(p_n, KC)
            for o in range(KC):
                pool.wait_ge(v_q, o + 1)
                link(TT(w1q[:, o], w1q[:, o], w1n[:, o], ALU.subtract))
                link(TT(w1q[:, o], w1q[:, o], w1n[:, o], ALU.add))
                link(TT(groups(w1q[:, o]), groups(w1q[:, o]), by_group(scale, o), ALU.mult))
                TT(w1q[:, o], w1q[:, o], delta[:, o], ALU.add).then_inc(p_w, 1)

            def split(pairs, done):
                for hi, lo, raw in pairs:
                    last = copy(hi, raw)
                link(last)
                for hi, lo, raw in pairs:
                    last = TT(lo, raw, hi.bitcast(F32), ALU.subtract)
                last.then_inc(done, 1)

            def split_ag(h):
                pool.wait_ge(ld_ag, 16 * NB)
                split([(ag[:, b // 2, c, :, b % 2, 0], ag[:, b // 2, c, :, b % 2, 1], agr[:, b, c])
                       for b in range(HB * h, HB * (h + 1)) for c in range(KC)], p_ag)

            def split_b3(h):
                for b in range(HB * h, HB * (h + 1)):
                    raw = b3r[:, b]
                    for g in (2, 3):
                        copy(b3[:, :, b, g], raw)
                    link(copy(b3[:, :, b, 0], raw))
                    last = TT(b3[:, :, b, 1], raw, b3[:, :, b, 0].bitcast(F32), ALU.subtract)
                last.then_inc(p_b3, 1)

            def stack_b(h, dst, raw, ld, done):
                pool.wait_ge(ld, 16 * HB * (h + 1))
                out = dst[:, 2 * h:2 * h + 2]
                link(copy(out, raw[:]))
                for p in range(2):
                    link(nc.gpsimd.tensor_scalar(b_part[:], out[:, p].bitcast(F32), minus_b_lo, None, ALU.mult))
                    last = TT(out[:, p], raw[:, p], b_part[:], ALU.add)
                    if p == 0:
                        link(last)
                last.then_inc(done, 1)
                pool.wait_ge(done, h + 1)

            def split_ad(q, s, j, h):
                pool.wait_ge(ld_ad, 16 * NB)
                if not (isinstance(q, int) and q == 0):
                    pool.wait_ge(s_d, 2 * q + s - 1)
                copy(ad[:, s, :, 0], ad_raw(j, h))
                copy(ad[:, s, :, 2], ad_raw(j, h))
                copy(ad[:, s, :, 3], ad_raw(j, h)).then_inc(p_ad, 1)

            split_ag(0)
            split_ag(1)
            stack_b(0, bd, bdr, ld_bd, p_bd)
            stack_b(0, a3, a3r, ld_a3, p_a3)
            pool.wait_ge(ld_b3, 16 * NB)
            pool.wait_ge(s_l0, 2 * KC)
            split_b3(0)
            split_b3(1)
            pool.wait_ge(s_w1t, KC)
            for h in range(2):
                n0 = NJ * h

                def at(j):
                    return (n0 + j) // 2, (n0 + j) % 2

                for j in range(3):
                    split_ad(*at(j), j, h)
                with pool.Fori(0, 3) as i:
                    for k in range(2):
                        q, s = at(3 + k)
                        split_ad(q + i, s, 3 + k + 2 * i, h)
                for j in (9, 10):
                    split_ad(*at(j), j, h)
                if h == 0:
                    stack_b(1, bd, bdr, ld_bd, p_bd)
                    stack_b(1, a3, a3r, ld_a3, p_a3)


def kernel(**inputs):
    import numpy as np
    import concourse.bacc as bacc
    from concourse import mybir as mb
    from concourse.bass_utils import run_bass_kernel_spmd as run

    a = {k: np.asarray(v) for k, v in inputs.items()}

    def pad_f(m, axis):
        width = [(0, 0)] * m.ndim
        width[axis] = (0, FP - F)
        return np.pad(m, width)

    def gate_up(wg, wu):
        w = np.stack([pad_f(wg, 0), pad_f(wu, 0)])
        return w.reshape(2, NJ, P, KC, P).transpose(1, 4, 0, 3, 2).reshape(NJ, P, 2 * KC * P)

    row, col = np.arange(P)[:, None], np.arange(H)[None]
    consts = np.concatenate([
        np.eye(P), 0.5 * (row // (2 * R) % 2 == col // BT % 2), 0.5 * (row // (G4 * R) == col // BT % 2),
        np.arange(E) + 0 * row, E - np.arange(E) + 0 * row, -1.0 * (row // R % G4 == 2),
        -1.0 * (row // R % G4 == 3)], axis=1).astype(np.float32)
    na = a["L2_cond_A_gate"].shape[1]
    ag = np.stack([a["L2_cond_A_gate"][0], a["L2_cond_A_up"][0]])
    bg = np.stack([pad_f(a["L2_cond_B_gate"][0], 1), pad_f(a["L2_cond_B_up"][0], 1)])
    adn = pad_f(a["L2_cond_A_down"][0], 2)
    arrays = {
        "x": a["x"].reshape(TOK, D).T,
        "aw": np.concatenate([a["L0_cond_A"].reshape(E * R, D), a["L0_cond_Wr"]]).T,
        "w0": a["L0_cond_W"].T,
        "b0": a["L0_cond_B"].transpose(0, 2, 1).reshape(E * R, D),
        "w1": a["L1_cond_weight"],
        "slog": a["L1_cond_scale_log"].reshape(D, KC),
        "la1": a["L1_cond_lora_A"],
        "lb1": a["L1_cond_lora_B"].T,
        "cb": a["condB_codebook"],
        "lang": a["itok_B_0_7"],
        "idx2": a["itok_B_2_6"].reshape(1, NB),
        "idx3": a["itok_B_3_7"].reshape(1, NB),
        "wgu": gate_up(a["L2_cond_W_gate"], a["L2_cond_W_up"]),
        "wd": pad_f(a["L2_cond_W_down"], 1).T.reshape(NJ, P, D),
        "agu": ag.reshape(2, na, R, KC, P).transpose(1, 4, 3, 0, 2).reshape(na, P, KC * 2 * R),
        "bgu": bg.reshape(2, na, NJ, P, R).transpose(1, 2, 4, 0, 3).reshape(na, NJ, R, 2 * P),
        "ad": adn.reshape(na, R, NJ, P).transpose(0, 3, 2, 1).reshape(na, P, NJ * R),
        "bd": a["L2_cond_B_down"][0].transpose(0, 2, 1),
        "a3": a["L3_cond_A"].transpose(0, 2, 1),
        "b3": a["L3_cond_B"].reshape(-1, R, KC, P).transpose(0, 3, 2, 1).reshape(-1, P, KC * R),
        "consts": consts,
    }
    nc = bacc.Bacc("TRN2", target_bir_lowering=False, num_devices=1)
    feeds, aps = {}, {}
    for name, v in arrays.items():
        v = np.ascontiguousarray(v)
        feeds[name + "_dram"] = v
        aps[name] = nc.dram_tensor(name + "_dram", v.shape, mb.dt.from_np(v.dtype), kind="ExternalInput").ap()
    aps["out"] = nc.dram_tensor("out_dram", (D, TOK), mb.dt.float32, kind="ExternalOutput").ap()
    program(nc, aps)
    r = run(nc, [feeds], core_ids=[0])
    return np.ascontiguousarray(r.results[0]["out_dram"].T).reshape(NB, BT, D)
```

```python
from contextlib import ExitStack

import concourse.bass as bass
from concourse import mybir

ALU = mybir.AluOpType
ACT = mybir.ActivationFunctionType
AX_X = mybir.AxisListType.X
F32 = mybir.dt.float32
F32R = mybir.dt.float32r
I32 = mybir.dt.int32

P = 128
D = 512
KC = D // P
NB = 8
BT = 128
TOK = NB * BT
H = TOK // 2
HB = NB // 2
E = 8
R = 16
R1 = 64
NCB = 8
F = 1376
NJ = -(-F // P)
FP = NJ * P
AW = E * R + E
G4 = 4
STACKED = 2 * G4 * R
UP_PARTS = 16 * 12

GATE, UP, TDOWN, SPARE, DOWN = 0, 1, 2, 3, 4


def program(nc, t):
    with ExitStack() as ctx:
        cursor = [-(-nc.sbuf_base // 64) * 64]

        def sb(name, shape, dt=F32, at=None):
            n = 4
            for s in shape[1:]:
                n *= s
            off = cursor[0] if at is None else at
            if at is None:
                cursor[0] += -(-n // 64) * 64
            return nc.alloc_sbuf_tensor_at(name, list(shape), dt, offset=off)

        def sem(name):
            return ctx.enter_context(nc.semaphore(name))

        ps = ctx.enter_context(nc.psum_tensor("ps", [P, 8, 512], F32))

        y = sb("y", [P, KC, TOK])
        y_hi = sb("y_hi", [P, KC, TOK], F32R)
        y_lo = sb("y_lo", [P, KC, TOK], F32R)

        aw = sb("aw", [P, KC, AW])
        consts = sb("consts", [P, P + 2 * H + 2 * E + 2])
        ident = consts[:, 0:P]
        e_iota = consts[:, P:P + E]
        e_rank = consts[:, P + E:P + 2 * E]
        minus_b_lo = consts[:, P + 2 * E:P + 2 * E + 1]
        minus_t_lo = consts[:, P + 2 * E + 1:P + 2 * E + 2]
        masks = P + 2 * E + 2
        up_mask = consts[:, masks:masks + H]
        pair_mask = consts[:, masks + H:masks + 2 * H]
        lang_i = sb("lang_i", [P, NB], I32)
        lang_f = sb("lang_f", [P, NB])
        bias = sb("bias", [P, NB, E])
        rt = sb("rt", [P, 6, NB, E])
        rs1 = sb("rs1", [P, 8, NB])
        gates = sb("gates", [P, NB, E])
        gated = sb("gated", [P, NB, E, R])
        gh_hi = sb("gh_hi", [P, TOK], F32R)
        gh_lo = sb("gh_lo", [P, TOK], F32R)
        early = cursor[0]
        lb1 = sb("lb1", [R1, D])
        la1 = sb("la1", [R1, D])
        b0 = sb("b0", [P, D])
        b0_hi = sb("b0_hi", [P, D], F32R)
        b0_lo = sb("b0_lo", [P, D], F32R)
        slog = sb("slog", [P, KC * KC])
        scale = sb("scale", [P, KC * KC])
        rscale = sb("rscale", [P, KC * KC])
        cbk = sb("cbk", [P, NCB])
        cbt = sb("cbt", [P, 6, NCB])

        c_abs, c_n, thr, u, step = (cbt[:, k] for k in range(5))

        region = cursor[0]
        w0 = sb("w0", [P, KC, D])
        w0_hi = sb("w0_hi", [P, KC, D], F32R)
        w0_lo = sb("w0_lo", [P, KC, D], F32R)
        w1q = sb("w1q", [P, KC, D])
        region2 = cursor[0]
        w1 = sb("w1", [P, KC, D])
        delta = sb("delta", [P, KC, D])
        w1n = sb("w1n", [P, KC, D])
        region_end = cursor[0]
        w1t_hi = sb("w1t_hi", [P, KC, KC, P], F32R, at=region2 + 2 * KC * D * 4)
        w1t_lo = sb("w1t_lo", [P, KC, KC, P], F32R)

        KB = 1024
        wgu_hi = sb("wgu_hi", [P, 2, 2, KC, P], F32R, at=region)
        wgu_lo = sb("wgu_lo", [P, 2, 2, KC, P], F32R, at=region + 8 * KB)
        wd_hi = sb("wd_hi", [P, 2, D], F32R, at=region + 16 * KB)
        wd_lo = sb("wd_lo", [P, 2, D], F32R, at=region + 20 * KB)
        bl = sb("bl", [P, 2, 2, 2, P], F32R, at=region + 24 * KB)
        ad = sb("ad", [P, 2, HB, G4, R], F32R, at=region + 28 * KB)
        act_hi = sb("act_hi", [P, 2, H], F32R, at=region2 + 16 * KB)
        act_lo = sb("act_lo", [P, 2, H], F32R, at=region2 + 20 * KB)
        act = sb("act", [P, 2, H], at=region2 + 24 * KB)
        silu_g = sb("silu_g", [P, 2, H], at=region2 + 28 * KB)
        tg = sb("tg", [P, 2, H], F32R, at=region2)
        tu = sb("tu", [P, 2, H], F32R, at=region2 + 4 * KB)
        td = sb("td", [P, H], F32R, at=region2 + 8 * KB)
        tm = sb("tm", [P, H], at=region2 + 10 * KB)
        t_hi = sb("t_hi", [P, H], F32R, at=region2 + 12 * KB)
        t_lo = sb("t_lo", [P, H], F32R, at=region2 + 14 * KB)

        wgu = sb("wgu", [P, 2, 2, KC, P])
        wd = sb("wd", [P, 2, D])
        blr = sb("blr", [P, 2, 2, 2, P])
        agr = sb("agr", [P, NB, KC, 2, R])
        ag = sb("ag", [P, 4, KC, 2, 2, 2, R], F32R)
        adr = sb("adr", [P, NB, NJ, R])
        bdr = sb("bdr", [P, 2, D])
        bd = sb("bd", [P, 4, D], F32R)
        a3r = sb("a3r", [P, 2, D])
        a3 = sb("a3", [P, 4, D], F32R)
        b3r = sb("b3r", [P, NB, KC, R])
        b_part = sb("b_part", [P, D])
        b3 = sb("b3", [P, KC, NB, G4, R], F32R, at=early)
        idx = sb("idx", [1, 2 * NB], I32)
        assert cursor[0] <= nc.sbuf_usable_end

        ld_aw, ld_l1, ld_c, ld_masks, ld_small, ld_w1, ld_w0, ld_b0, ld_idx = (
            sem(n) for n in ("ld_aw", "ld_l1", "ld_c", "ld_masks", "ld_small", "ld_w1", "ld_w0", "ld_b0", "ld_idx"))
        ld_x = [sem("ld_x0"), sem("ld_x1")]
        ld_ag, ld_ad, ld_b3 = sem("ld_ag"), sem("ld_ad"), sem("ld_b3")
        ld_bd, ld_a3 = sem("ld_bd"), sem("ld_a3")
        ld_wgu = [sem("ld_wgu0"), sem("ld_wgu1")]
        ld_wd = [sem("ld_wd0"), sem("ld_wd1")]
        ld_bl = [sem("ld_bl0"), sem("ld_bl1")]
        ld_t, st_out = sem("ld_t"), sem("st_out")
        s_delta, s_hlog, s_l0, s_ght, s_w1t, s_l1 = (
            sem(n) for n in ("s_delta", "s_hlog", "s_l0", "s_ght", "s_w1t", "s_l1"))
        s_ta, s_g, s_u, s_d, s_td, s_dn, s_t3, s_o3 = (
            sem(n) for n in ("s_ta", "s_g", "s_u", "s_d", "s_td", "s_dn", "s_t3", "s_o3"))
        a_dc, a_es, a_exp, a_yh, a_w0, a_b0, a_gh, a_w1t = (
            sem(n) for n in ("a_dc", "a_es", "a_exp", "a_yh", "a_w0", "a_b0", "a_gh", "a_w1t"))
        a_th, a_silu, a_ah, a_wg, a_wd, a_bl = (sem(n) for n in ("a_th", "a_silu", "a_ah", "a_wg", "a_wd", "a_bl"))
        v_chain, v_rs, v_cb, v_dm, v_gate, v_y, v_yl, v_w0, v_gh, v_q, v_w1t = (
            sem(n) for n in ("v_chain", "v_rs", "v_cb", "v_dm", "v_gate", "v_y", "v_yl", "v_w0",
                             "v_gh", "v_q", "v_w1t"))
        v_step, a_step, p_yl, p_b0, v_w = (sem(n) for n in ("v_step", "a_step", "p_yl", "p_b0", "v_w"))
        v_tm, v_tl, v_act, v_al, v_wg, v_wd, v_ad, v_bl, v_out = (
            sem(n) for n in ("v_tm", "v_tl", "v_act", "v_al", "v_wg", "v_wd", "v_ad", "v_bl", "v_out"))
        p_chain, p_n, p_w, p_ag, p_ad, p_bd, p_a3, p_b3 = (
            sem(n) for n in ("p_chain", "p_n", "p_w", "p_ag", "p_ad", "p_bd", "p_a3", "p_b3"))

        def half(h):
            return slice(h * H, (h + 1) * H)

        y_lo_by = {0: (v_yl, KC), 1: (p_yl, KC), 2: (p_yl, 2 * KC)}
        y_lo_by.update({v: (v_yl, KC * (v - 1)) for v in range(3, 7)})

        w1_by = ((p_w, 1), (p_w, 2), (v_w, 1), (p_w, 3))

        last_y_lo = ((p_yl, 2 * KC + 1), (v_yl, 5 * KC + 1), (p_yl, 2 * KC + 2), (v_yl, 5 * KC + 2))

        quant_order = [(k, o) for pair in ((0, 1), (2, 3)) for k in range(6, 0, -1) for o in pair]

        def ad_raw(j, h):
            return adr[:, HB * h:HB * (h + 1), bass.ds(j, 1), :].rearrange("p b j r -> p b (j r)")

        block = ctx.enter_context(nc.Block())

        @block.sync
        def _(sp):
            def chunks(ap):
                return ap.rearrange("(c p) n -> p c n", p=P)

            xv, w1v, w0v = chunks(t["x"]), chunks(t["w1"]), chunks(t["w0"])
            sp.dma_start(lb1[:], t["lb1"]).then_inc(ld_l1, 16)
            sp.dma_start(la1[:], t["la1"]).then_inc(ld_l1, 16)
            sp.dma_start(slog[:].rearrange("p (c g) -> p c g", g=KC), chunks(t["slog"])).then_inc(ld_small, 16)
            sp.dma_start(cbk[:], t["cb"].partition_broadcast(P)).then_inc(ld_small, 16)
            sp.dma_start(lang_i[:], t["lang"].partition_broadcast(P)).then_inc(ld_small, 16)
            sp.dma_start(aw[:], chunks(t["aw"])).then_inc(ld_aw, 16)
            sp.dma_start(consts[:, 0:masks], t["consts"][:, 0:masks]).then_inc(ld_c, 16)
            for c in range(0, KC, 2):
                sp.dma_start(y[:, c:c + 2, half(0)], xv[:, c:c + 2, half(0)]).then_inc(ld_x[0], 16)
            for c in range(0, KC, 2):
                sp.dma_start(w0[:, c:c + 2], w0v[:, c:c + 2]).then_inc(ld_w0, 16)
            for c in range(0, KC, 2):
                sp.dma_start(w1[:, c:c + 2], w1v[:, c:c + 2]).then_inc(ld_w1, 16)
            for c in range(0, KC, 2):
                sp.dma_start(y[:, c:c + 2, half(1)], xv[:, c:c + 2, half(1)]).then_inc(ld_x[1], 16)
            sp.dma_start(b0[:], t["b0"]).then_inc(ld_b0, 16)
            sp.dma_start(idx[:, 0:NB], t["idx2"]).then_inc(ld_idx, 16)
            sp.dma_start(idx[:, NB:2 * NB], t["idx3"]).then_inc(ld_idx, 16)
            sp.dma_start(consts[:, masks:], t["consts"][:, masks:]).then_inc(ld_masks, 16)
            sp.wait_ge(ld_idx, 32)

            def adapter2(b):
                return sp.value_load(idx[0:1, b:b + 1], min_val=0, max_val=15)

            def adapter3(b):
                return sp.value_load(idx[0:1, NB + b:NB + b + 1], min_val=0, max_val=7)

            def grouped(tile_ap, b2):
                return tile_ap[b2 * G4 * R:(b2 + 1) * G4 * R]

            def repeated(ap):
                r, n = ap.shape
                return ap.unsqueeze(0).to_broadcast([G4, r, n])

            def load_a(b):
                sp.dma_start(agr[:, b], t["agu"][bass.ds(adapter2(b), 1)].rearrange("a p n -> (a p) n")).then_inc(ld_ag, 16)

            def load_ad(b):
                sp.dma_start(adr[:, b], t["ad"][bass.ds(adapter2(b), 1)].rearrange("a p n -> (a p) n")).then_inc(ld_ad, 16)

            def load_b3(b):
                i3 = adapter3(b)
                sp.dma_start(b3r[:, b], t["b3"][bass.ds(i3, 1)].rearrange("a p n -> (a p) n")).then_inc(ld_b3, 16)

            def load_bd_a3(h):
                if h == 1:
                    sp.wait_ge(p_bd, 2)
                    sp.wait_ge(p_a3, 2)
                for b in range(HB):
                    i2 = adapter2(HB * h + b)
                    i3 = adapter3(HB * h + b)
                    sp.dma_start(grouped(bdr[:, b // 2], b % 2),
                                 repeated(t["bd"][bass.ds(i2, 1)].rearrange("a r n -> (a r) n"))).then_inc(ld_bd, 16)
                    sp.dma_start(grouped(a3r[:, b // 2], b % 2),
                                 repeated(t["a3"][bass.ds(i3, 1)].rearrange("a r n -> (a r) n"))).then_inc(ld_a3, 16)

            def load_wgu(j, q, s, h):
                if not (isinstance(q, int) and q == 0):
                    sp.wait_ge(a_wg, 2 * q + s - 1)
                    sp.wait_ge(v_wg, 2 * q + s - 1)
                    sp.wait_ge(v_bl, 2 * q + s - 1)
                sp.dma_start(wgu[:, s], t["wgu"][bass.ds(j, 1)].rearrange("j p n -> (j p) n")).then_inc(ld_wgu[s], 16)
                for b in range(HB):
                    src = t["bgu"][bass.ds(bl_idx[HB * h + b], 1), bass.ds(j, 1)].rearrange("a j r n -> (a j r) n")
                    sp.dma_start(grouped(blr[:, s, b // 2].rearrange("p u f -> p (u f)"), b % 2),
                                 repeated(src)).then_inc(ld_bl[s], 16)

            def load_wd(j, q, s):
                if not (isinstance(q, int) and q == 0):
                    sp.wait_ge(a_wd, 2 * q + s - 1)
                    sp.wait_ge(v_wd, 2 * q + s - 1)
                sp.dma_start(wd[:, s], t["wd"][bass.ds(j, 1)].rearrange("j p n -> (j p) n")).then_inc(ld_wd[s], 16)

            def stack_up(h):
                sp.wait_ge(a_th, h + 1)
                sp.wait_ge(v_tl, h + 1)
                for u, dst in enumerate((tg, tu)):
                    for b in range(2):
                        to, row = b * G4 * R, (u * 2 + b) * 2 * R
                        for src, rows, at_ in ((t_hi, 2 * R, 0), (t_hi, R, 2 * R), (t_lo, R, 3 * R)):
                            sp.dma_start(dst[to + at_:to + at_ + rows, h].bitcast(F32),
                                            src[row:row + rows].bitcast(F32)).then_inc(ld_t, 16)

            bl_idx = {b: adapter2(b) for b in range(HB)}
            load_wgu(0, 0, 0, 0)
            load_wgu(1, 0, 1, 0)
            for b in range(NB):
                load_a(b)
            load_wd(0, 0, 0)
            for b in range(NB):
                load_ad(b)
            load_bd_a3(0)
            for b in range(NB):
                load_b3(b)
            for h in range(2):
                n0 = NJ * h
                if h == 1:
                    load_wd(0, n0 // 2, n0 % 2)
                load_wgu(2, (n0 + 2) // 2, n0 % 2, h)
                for j in (1, 2):
                    n = n0 + j
                    load_wd(j, n // 2, n % 2)
                    if h == 0:
                        stack_up(j - 1)
                    load_wgu(j + 2, (n + 2) // 2, n % 2, h)
                if h == 1:
                    load_bd_a3(1)
                with sp.Fori(0, 3) as i:
                    for k in range(2):
                        n = n0 + 3 + k
                        load_wd(3 + k + 2 * i, n // 2 + i, n % 2)
                        load_wgu(5 + k + 2 * i, (n + 2) // 2 + i, n % 2, h)
                if h == 0:
                    bl_idx.update({b: adapter2(b) for b in range(HB, NB)})
                for j in (9, 10):
                    n = n0 + j
                    load_wd(j, n // 2, n % 2)
                    if h == 0:
                        load_wgu(j - 9, (n + 2) // 2, n % 2, 1)
            ov = t["out"].rearrange("(c p) n -> p c n", p=P)
            for h in range(2):
                for c in range(KC):
                    sp.wait_ge(v_out, KC * h + c + 1)
                    sp.dma_start(ov[:, c, half(h)], y[:, c, half(h)]).then_inc(st_out, 16)
            sp.wait_ge(st_out, 16 * 2 * KC)

        @block.tensor
        def _(pe):
            def three(out, w_hi, w_lo, r_hi, r_lo, start, stop):
                nc.tensor.matmul(out, w_hi, r_hi, start=start, stop=False, skip_group_check=True)
                nc.tensor.matmul(out, w_hi, r_lo, start=False, stop=False, skip_group_check=True)
                return nc.tensor.matmul(out, w_lo, r_hi, start=False, stop=stop, skip_group_check=True)

            def y_ready(group):
                pe.wait_ge(a_yh, KC * (group + 1))
                pe.wait_ge(*y_lo_by[group])

            pe.wait_ge(ld_l1, 32)
            for o in range(KC):
                nc.tensor.matmul(ps[:, o], lb1[:, o * P:(o + 1) * P], la1[:], start=True, stop=True).then_inc(s_delta, 1)

            def router(h):
                pe.wait_ge(ld_x[h], 32)
                for b in range(HB * h, HB * (h + 1)):
                    out = ps[:, 4 + b // 2, (b % 2) * AW:(b % 2 + 1) * AW]
                    for c in range(KC):
                        last = nc.tensor.matmul(out, y[:, c, b * BT:(b + 1) * BT], aw[:, c],
                                                start=(c == 0), stop=(c == KC - 1))
                    if b % 2:
                        last.then_inc(s_hlog, 1)

            pe.wait_ge(ld_aw, 16)
            router(0)

            def l0_base(h, o):
                for c in range(KC):
                    three(ps[:, 4 * h + o], w0_hi[:, c, o * P:(o + 1) * P], w0_lo[:, c, o * P:(o + 1) * P],
                          y_hi[:, c, half(h)], y_lo[:, c, half(h)], c == 0, False)

            def l0_lora(h):
                pe.wait_ge(a_b0, 1)
                pe.wait_ge(p_b0, 1)
                pe.wait_ge(a_gh, h + 1)
                pe.wait_ge(v_gh, h + 1)
                for o in range(KC):
                    three(ps[:, 4 * h + o], b0_hi[:, o * P:(o + 1) * P], b0_lo[:, o * P:(o + 1) * P],
                          gh_hi[:, half(h)], gh_lo[:, half(h)], False, True).then_inc(s_l0, 1)

            y_ready(0)
            pe.wait_ge(a_w0, KC)
            pe.wait_ge(v_w0, KC)
            pe.wait_ge(a_dc, KC)
            l0_base(0, 0)
            router(1)
            for o in range(1, KC):
                l0_base(0, o)
            pe.wait_ge(ld_c, 16)
            pe.wait_ge(v_gate, 1)
            for b in range(NB):
                last = nc.tensor.transpose(ps[:, 4 + b // HB, b % HB * BT:(b % HB + 1) * BT],
                                           gated[:, b].rearrange("p e r -> p (e r)"), ident)
                if b % HB == HB - 1:
                    last.then_inc(s_ght, 1)
            y_ready(1)
            l0_base(1, 2)
            l0_lora(0)
            l0_base(1, 3)
            pe.wait_ge(a_gh, 2)
            pe.wait_ge(v_gh, 2)
            l0_base(1, 0)
            l0_base(1, 1)

            def w1_transpose(o):
                pe.wait_ge(v_y, o + 1)
                pe.wait_ge(*w1_by[o])
                for c in range(KC):
                    last = nc.tensor.transpose(ps[:, o, c * P:(c + 1) * P], w1q[:, o, c * P:(c + 1) * P], ident)
                last.then_inc(s_w1t, 1)

            w1_transpose(0)
            w1_transpose(1)
            l0_lora(1)

            def l1(h, o):
                pe.wait_ge(a_w1t, o + 1)
                pe.wait_ge(v_w1t, o + 1)
                for c in range(KC):
                    last = three(ps[:, 4 * h + o], w1t_hi[:, o, c], w1t_lo[:, o, c],
                                 y_hi[:, c, half(h)], y_lo[:, c, half(h)], c == 0, c == KC - 1)
                last.then_inc(s_l1, 1)

            def t_up(h):
                y_ready(4 + h)
                pe.wait_ge(p_ag, h + 1)
                for p in range(2):
                    out = ps[:, SPARE, p * 2 * BT:(p + 1) * 2 * BT]
                    cols = slice(h * H + p * 2 * BT, h * H + (p + 1) * 2 * BT)
                    for c in range(KC):
                        w = ag[:, 2 * h + p, c].rearrange("p u b s r -> p (u b s r)")
                        nc.tensor.matmul(out, w, y_hi[:, c, cols], start=(c == 0), stop=False, skip_group_check=True)
                        last = nc.tensor.matmul(out, w, y_lo[:, c, cols], start=False, stop=(c == KC - 1), skip_group_check=True)
                last.then_inc(s_ta, 1)

            y_ready(2)
            l1(0, 0)
            l1(0, 1)
            w1_transpose(2)
            w1_transpose(3)
            l1(0, 2)
            l1(0, 3)
            y_ready(3)
            l1(1, 0)
            t_up(0)
            l1(1, 1)
            l1(1, 2)
            l1(1, 3)

            def gate_or_up(which, bank, s, h, done):
                for c in range(KC):
                    three(ps[:, bank], wgu_hi[:, s, which, c], wgu_lo[:, s, which, c],
                          y_hi[:, c, half(h)], y_lo[:, c, half(h)], c == 0, False)
                pe.wait_ge(ld_t, UP_PARTS * (h + 1))
                tt = tg if which == 0 else tu
                for p in range(2):
                    last = nc.tensor.matmul(ps[:, bank, p * 2 * BT:(p + 1) * 2 * BT], bl[:, s, p, which],
                                            tt[:, h, p * 2 * BT:(p + 1) * 2 * BT], start=False, stop=(p == 1),
                                            skip_group_check=True)
                last.then_inc(done, 1)

            def gate(q, s, h, first=False):
                n = 2 * q + s
                pe.wait_ge(a_wg, n + 1)
                pe.wait_ge(v_wg, n + 1)
                pe.wait_ge(v_bl, n + 1)
                if not first:
                    pe.wait_ge(a_silu, n)
                gate_or_up(0, GATE, s, h, s_g)

            def up(q, s, h, first=False):
                if not first:
                    pe.wait_ge(v_act, 2 * q + s)
                gate_or_up(1, UP, s, h, s_u)

            def t_down(q, s, first):
                n = 2 * q + s
                pe.wait_ge(a_ah, n + 1)
                pe.wait_ge(v_al, n + 1)
                pe.wait_ge(p_ad, n + 1)
                pe.wait_ge(v_ad, n + 1)
                for p in range(2):
                    cols = slice(p * 2 * BT, (p + 1) * 2 * BT)
                    out = ps[:, TDOWN, cols]
                    w = ad[:, s, 2 * p:2 * p + 2].rearrange("p b g r -> p (b g r)")
                    nc.tensor.matmul(out, w, act_hi[:, s, cols], start=(first and p == 0), stop=False,
                                     skip_group_check=True)
                    last = nc.tensor.matmul(out, w, act_lo[:, s, cols], start=False, stop=False,
                                            skip_group_check=True)
                return last

            def down(q, s, first=False):
                n = 2 * q + s
                pe.wait_ge(a_wd, n + 1)
                pe.wait_ge(v_wd, n + 1)
                for o in range(KC):
                    last = three(ps[:, DOWN + o], wd_hi[:, s, o * P:(o + 1) * P], wd_lo[:, s, o * P:(o + 1) * P],
                                 act_hi[:, s], act_lo[:, s], first, False)
                last.then_inc(s_d, 1)

            def down_lora(h):
                pe.wait_ge(p_bd, 2 * (h + 1))
                pe.wait_ge(v_tl, 3 + 2 * h)
                for o in range(KC):
                    for p in range(2):
                        cols = slice(p * 2 * BT, (p + 1) * 2 * BT)
                        last = nc.tensor.matmul(ps[:, DOWN + o, cols], bd[:, 2 * h + p, o * P:(o + 1) * P], td[:, cols],
                                                start=False, stop=(p == 1), skip_group_check=True)
                    last.then_inc(s_dn, 1)

            def t_three(h):
                pe.wait_ge(p_b3, h + 1)
                if h == 0:
                    y_ready(6)
                for c in range(KC):
                    for part, y_part in enumerate((y_hi, y_lo)):
                        if h == 1 and part == 0:
                            pe.wait_ge(a_yh, KC * 7 + c + 1)
                        if h == 1 and part == 1:
                            by, n = last_y_lo[c]
                            pe.wait_ge(by, n)
                        for p in range(2):
                            w = b3[:, c, HB * h + 2 * p:HB * h + 2 * p + 2].rearrange("p b g r -> p (b g r)")
                            cols = slice(h * H + p * 2 * BT, h * H + (p + 1) * 2 * BT)
                            last = nc.tensor.matmul(ps[:, SPARE, p * 2 * BT:(p + 1) * 2 * BT], w, y_part[:, c, cols],
                                                    start=(c == 0 and part == 0 and p == 0), stop=(c == KC - 1 and part == 1),
                                                    skip_group_check=True)
                last.then_inc(s_t3, 1)

            def out_three(h, o, bank):
                if h == 0 and o > 0:
                    pe.wait_ge(v_out, o)
                pe.wait_ge(p_a3, 2 * (h + 1))
                pe.wait_ge(v_tl, 4 + 2 * h)
                for p in range(2):
                    cols = slice(p * 2 * BT, (p + 1) * 2 * BT)
                    last = nc.tensor.matmul(ps[:, bank, cols], a3[:, 2 * h + p, o * P:(o + 1) * P], td[:, cols],
                                            start=(p == 0), stop=True, skip_group_check=True)
                last.then_inc(s_o3, 1)

            for h in range(2):
                n0 = NJ * h

                def at(j):
                    return (n0 + j) // 2, (n0 + j) % 2

                y_ready(4 + h)
                gate(*at(0), h, first=(h == 0))
                if h == 1:
                    down_lora(0)
                up(*at(0), h, first=(h == 0))
                if h == 0:
                    pe.wait_ge(v_tm, 1)
                    t_up(1)
                gate(*at(1), h)
                up(*at(1), h)
                if h == 1:
                    t_three(0)
                pe.wait_ge(v_y, KC * (4 if h == 0 else 5))
                if h == 1:
                    pe.wait_ge(v_tm, 3)
                t_down(*at(0), True)
                down(*at(0), first=True)
                gate(*at(2), h)
                if h == 1:
                    pe.wait_ge(v_tm, 4)
                    out_three(0, 0, SPARE)
                up(*at(2), h)
                if h == 1:
                    out_three(0, 1, SPARE)
                t_down(*at(1), False)
                down(*at(1))
                if h == 1:
                    out_three(0, 2, SPARE)
                with pe.Fori(0, 4) as i:
                    for k in range(2):
                        q, s = at(3 + k)
                        gate(q + i, s, h)
                        up(q + i, s, h)
                        q, s = at(2 + k)
                        t_down(q + i, s, False)
                        down(q + i, s)
                if h == 1:
                    out_three(0, 3, SPARE)
                t_down(*at(NJ - 1), False).then_inc(s_td, 1)
                down(*at(NJ - 1))
            down_lora(1)
            pe.wait_ge(v_out, KC)
            t_three(1)
            pe.wait_ge(v_tm, 6)
            for o in range(KC):
                out_three(1, o, (GATE, UP, TDOWN, SPARE)[o])

        @block.scalar
        def _(act_e):
            def cast(out, in_):
                return nc.scalar.activation(out, in_, ACT.Copy)

            def split_y(h, c):
                return cast(y_hi[:, c, half(h)], y[:, c, half(h)]).then_inc(a_yh, 1)

            def result_hi(layer, h):
                if layer < 2:
                    act_e.wait_ge((s_l0, s_l1)[layer], KC * (h + 1))
                for c in range(KC):
                    act_e.wait_ge(v_y, KC * (2 * layer + h) + c + 1)
                    split_y(h, c)

            def quant_add(events):
                for k, o in events:
                    act_e.wait_ge(v_step, quant_order.index((k, o)) + 1)
                    nc.scalar.activation(w1q[:, o], w1q[:, o], ACT.Identity, bias=step[:, k - 1:k]).then_inc(a_step, 1)

            act_e.wait_ge(ld_small, 48)
            nc.scalar.activation(scale[:], slog[:], ACT.Exp).then_inc(a_es, 1)
            for o in range(KC):
                act_e.wait_ge(s_delta, o + 1)
                nc.scalar.activation(delta[:, o], ps[:, o], ACT.Copy, scale=0.5).then_inc(a_dc, 1)
            act_e.wait_ge(ld_x[0], 32)
            for c in range(KC):
                split_y(0, c)
            act_e.wait_ge(ld_w0, 32)
            for c in range(KC):
                cast(w0_hi[:, c], w0[:, c]).then_inc(a_w0, 1)
            quant_add(quant_order[0:2])
            act_e.wait_ge(ld_x[1], 32)
            split_y(1, 0)
            split_y(1, 1)
            quant_add(quant_order[2:4])
            split_y(1, 2)
            split_y(1, 3)
            quant_add(quant_order[4:6])
            act_e.wait_ge(ld_b0, 16)
            cast(b0_hi[:], b0[:]).then_inc(a_b0, 1)
            act_e.wait_ge(v_dm, 1)
            nc.scalar.activation(rs1[:, 3], rs1[:, 2], ACT.Exp).then_inc(a_exp, 1)
            quant_add(quant_order[6:10])
            for h in range(2):
                act_e.wait_ge(s_ght, h + 1)
                cast(gh_hi[:, half(h)], ps[:, 4 + h]).then_inc(a_gh, 1)
                quant_add(quant_order[10 + 2 * h:12 + 2 * h])
            result_hi(0, 0)
            quant_add(quant_order[14:])

            def w1t_split(o):
                act_e.wait_ge(s_w1t, o + 1)
                cast(w1t_hi[:, o].rearrange("p c n -> p (c n)"), ps[:, o]).then_inc(a_w1t, 1)

            w1t_split(0)
            w1t_split(1)
            result_hi(0, 1)
            w1t_split(2)
            w1t_split(3)

            def split_wgu(q, s):
                n = 2 * q + s
                if not (isinstance(q, int) and q == 0):
                    act_e.wait_ge(s_u, n - 1)
                act_e.wait_ge(ld_wgu[s], 16 * (q + 1))
                cast(wgu_hi[:, s].rearrange("p u c f -> p (u c f)"),
                     wgu[:, s].rearrange("p u c f -> p (u c f)")).then_inc(a_wg, 1)
                act_e.wait_ge(ld_bl[s], 16 * HB * (q + 1))
                cast(bl[:, s].rearrange("p a u f -> p (a u f)"),
                     blr[:, s].rearrange("p a u f -> p (a u f)")).then_inc(a_bl, 1)

            def split_wd(q, s):
                n = 2 * q + s
                if not (isinstance(q, int) and q == 0):
                    act_e.wait_ge(s_d, n - 1)
                act_e.wait_ge(ld_wd[s], 16 * (q + 1))
                cast(wd_hi[:, s], wd[:, s]).then_inc(a_wd, 1)

            act_e.wait_ge(s_l0, 2 * KC)
            split_wgu(0, 0)
            result_hi(1, 0)

            def silu(q, s):
                n = 2 * q + s
                act_e.wait_ge(s_g, n + 1)
                if not (isinstance(q, int) and q == 0):
                    act_e.wait_ge(v_act, n - 1)
                nc.scalar.activation(silu_g[:, s], ps[:, GATE], ACT.Silu).then_inc(a_silu, 1)

            def act_split(q, s):
                n = 2 * q + s
                act_e.wait_ge(v_act, n + 1)
                if not (isinstance(q, int) and q == 0):
                    act_e.wait_ge(s_d, n - 1)
                cast(act_hi[:, s], act[:, s]).then_inc(a_ah, 1)

            def ranks_hi(k):
                act_e.wait_ge(v_tm, k)
                cast(t_hi[:], tm[:]).then_inc(a_th, 1)

            ranks_hi(1)
            split_wgu(0, 1)
            result_hi(1, 1)
            for h in range(2):
                n0 = NJ * h

                def at(j):
                    return (n0 + j) // 2, (n0 + j) % 2

                split_wd(*at(0))
                silu(*at(0))
                if h == 1:
                    result_hi(2, 0)
                act_split(*at(0))
                if h == 0:
                    act_e.wait_ge(ld_t, UP_PARTS)
                    ranks_hi(2)
                split_wgu(*at(2))
                split_wd(*at(1))
                silu(*at(1))
                act_split(*at(1))
                if h == 1:
                    ranks_hi(4)
                split_wgu(*at(3))
                silu(*at(2))
                split_wd(*at(2))
                act_split(*at(2))
                split_wgu(*at(4))
                with act_e.Fori(0, 3) as i:
                    for k in range(2):
                        q, s = at(3 + k)
                        split_wd(q + i, s)
                        silu(q + i, s)
                        act_split(q + i, s)
                        split_wgu(q + i + 1, s)
                for j in (9, 10):
                    split_wd(*at(j))
                    silu(*at(j))
                    act_split(*at(j))
                    if h == 0:
                        split_wgu(*at(j + 2))
                if h == 0:
                    act_e.wait_ge(ld_t, 2 * UP_PARTS)
                ranks_hi(3 + 2 * h)
            result_hi(2, 1)
            ranks_hi(6)

        @block.vector
        def _(dve):
            count = [0]

            def link(ins):
                count[0] += 1
                ins.then_inc(v_chain, 1)
                dve.wait_ge(v_chain, count[0])

            TT, TS = nc.vector.tensor_tensor, nc.vector.tensor_scalar

            def lo_of(out, whole, hi):
                return TT(out, whole, hi.bitcast(F32), ALU.subtract)

            def y_lo_of(group, h, c):
                dve.wait_ge(a_yh, KC * group + c + 1)
                lo_of(y_lo[:, c, half(h)], y[:, c, half(h)], y_hi[:, c, half(h)]).then_inc(v_yl, 1)

            dve.wait_ge(ld_small, 48)
            link(TS(c_abs, cbk[:], -1.0, None, ALU.mult))
            link(TT(c_abs, c_abs, cbk[:], ALU.max))
            link(nc.vector.tensor_reduce(cbt[:, 5, 0:1], c_abs, AX_X, ALU.max))
            link(TS(cbt[:, 5, 0:1], cbt[:, 5, 0:1], 1e-8, None, ALU.max))
            link(nc.vector.reciprocal(cbt[:, 5, 1:2], cbt[:, 5, 0:1]))
            link(TS(c_n, cbk[:], cbt[:, 5, 1:2], None, ALU.mult))
            TT(step[:, 0:7], c_n[:, 1:8], c_n[:, 0:7], ALU.subtract)
            link(TT(thr[:, 0:7], c_n[:, 1:8], c_n[:, 0:7], ALU.add))
            link(TS(thr[:, 0:7], thr[:, 0:7], 0.5, None, ALU.mult))
            link(nc.vector.tensor_copy(u[:, 3:4], thr[:, 3:4]))
            TT(u[:, 1:2], thr[:, 1:2], thr[:, 3:4], ALU.min)
            link(TT(u[:, 5:6], thr[:, 5:6], thr[:, 3:4], ALU.max))
            TT(u[:, 0:1], thr[:, 0:1], u[:, 1:2], ALU.min)
            TT(u[:, 6:7], thr[:, 6:7], u[:, 5:6], ALU.max)
            TT(c_abs[:, 2:3], thr[:, 2:3], u[:, 1:2], ALU.max)
            link(TT(c_abs[:, 4:5], thr[:, 4:5], u[:, 3:4], ALU.max))
            TT(u[:, 2:3], c_abs[:, 2:3], u[:, 3:4], ALU.min)
            link(TT(u[:, 4:5], c_abs[:, 4:5], u[:, 5:6], ALU.min))
            dve.wait_ge(a_es, 1)
            nc.vector.reciprocal(rscale[:], scale[:]).then_inc(v_rs, 1)
            link(nc.vector.tensor_copy(lang_f[:], lang_i[:]))
            dve.wait_ge(ld_c, 16)
            link(TT(bias[:], lang_f[:].unsqueeze(2).to_broadcast([P, NB, E]),
                    e_iota.unsqueeze(1).to_broadcast([P, NB, E]), ALU.is_equal))
            link(TS(bias[:], bias[:], 5.0, None, ALU.mult))

            def router_top2():
                dve.wait_ge(s_hlog, NB // 2)
                lg, eq, sc, oh1, lg2, oh2 = (rt[:, k] for k in range(6))
                m1, m2, first = rs1[:, 0], rs1[:, 1], rs1[:, 4]
                rank = e_rank.unsqueeze(1).to_broadcast([P, NB, E])
                link(TT(lg.rearrange("p (k b) e -> p k b e", b=2), bias[:].rearrange("p (k b) e -> p k b e", b=2),
                        hl[:, :, :, E * R:AW], ALU.add))
                link(nc.vector.tensor_reduce(m1, lg, AX_X, ALU.max))
                for src, m, oh in ((lg, m1, oh1), (lg2, m2, oh2)):
                    if src is lg2:
                        link(nc.vector.scalar_tensor_tensor(lg2, oh1, -3.0e38, lg, ALU.mult, ALU.add))
                        link(nc.vector.tensor_reduce(m2, lg2, AX_X, ALU.max))
                    link(TT(eq, src, wide(m), ALU.is_equal))
                    link(TT(sc, eq, rank, ALU.mult))
                    link(nc.vector.tensor_reduce(first, sc, AX_X, ALU.max))
                    link(TT(oh, rank, wide(first), ALU.is_equal))
                TT(rs1[:, 2], m2, m1, ALU.subtract).then_inc(v_dm, 1)

            hl = ps[:, 4:8, 0:2 * AW].rearrange("p k (b n) -> p k b n", b=2)

            def wide(v):
                return v.unsqueeze(2).to_broadcast([P, NB, E])

            def router_gates():
                oh1, oh2 = rt[:, 3], rt[:, 5]
                gap_exp, total, p1, p2 = rs1[:, 3], rs1[:, 5], rs1[:, 6], rs1[:, 7]
                dve.wait_ge(a_exp, 1)
                link(TS(total, gap_exp, 1.0, None, ALU.add))
                link(nc.vector.reciprocal(p1, total))
                link(TT(p2, gap_exp, p1, ALU.mult))
                TT(oh1, oh1, wide(p1), ALU.mult)
                link(TT(oh2, oh2, wide(p2), ALU.mult))
                link(TT(oh1, oh1, oh2, ALU.add))
                link(TS(gates[:], oh1, 2.0, None, ALU.mult))
                for k in range(NB // 2):
                    last = TT(gated[:, 2 * k:2 * k + 2], hl[:, k, :, 0:E * R].rearrange("p b (e r) -> p b e r", e=E),
                              gates[:, 2 * k:2 * k + 2].unsqueeze(3).to_broadcast([P, 2, E, R]), ALU.mult)
                last.then_inc(v_gate, 1)

            def quant_product(k, o):
                n, q = w1n[:, o], w1q[:, o]
                if k == 6:
                    dve.wait_ge(p_n, o + 1)
                    ins = TS(q, n, u[:, 6:7], step[:, 6:7], ALU.is_gt, ALU.mult)
                else:
                    dve.wait_ge(a_step, quant_order.index((k + 1, o)) + 1)
                    ins = nc.vector.scalar_tensor_tensor(q, n, u[:, k:k + 1], q, ALU.is_gt, ALU.mult)
                if (k, o) in quant_order:
                    ins.then_inc(v_step, 1)
                return ins

            def quant_last(o):
                return nc.vector.scalar_tensor_tensor(w1q[:, o], w1q[:, o], c_n[:, 0:1], w1n[:, o],
                                                      ALU.add, ALU.subtract)

            def gh_split(h):
                dve.wait_ge(a_gh, h + 1)
                lo_of(gh_lo[:, half(h)], ps[:, 4 + h], gh_hi[:, half(h)]).then_inc(v_gh, 1)

            for c in range(KC):
                y_lo_of(0, 0, c)
            for c in range(KC):
                dve.wait_ge(a_w0, c + 1)
                lo_of(w0_lo[:, c], w0[:, c], w0_hi[:, c]).then_inc(v_w0, 1)
            for k in (6, 5, 4):
                quant_product(k, 0)
                quant_product(k, 1)
            router_top2()
            quant_product(3, 0)
            quant_product(3, 1)
            router_gates()
            for k in (2, 1):
                quant_product(k, 0)
                quant_product(k, 1)
            gh_split(0)
            quant_product(0, 0)
            link(quant_product(0, 1))
            quant_last(0).then_inc(v_q, 1)
            gh_split(1)
            quant_last(1).then_inc(v_q, 1)
            quant_product(6, 2)
            quant_product(6, 3)

            def add_result(done, h, c, bank):
                dve.wait_ge(done, KC * h + c + 1)
                return TT(y[:, c, half(h)], y[:, c, half(h)], ps[:, bank], ALU.add)

            def w1t_split(o):
                dve.wait_ge(a_w1t, o + 1)
                lo_of(w1t_lo[:, o].rearrange("p c n -> p (c n)"), ps[:, o],
                      w1t_hi[:, o].rearrange("p c n -> p (c n)")).then_inc(v_w1t, 1)

            for c in range(KC):
                add_result(s_l0, 0, c, c).then_inc(v_y, 1)
            for k in range(5, 0, -1):
                quant_product(k, 2)
                quant_product(k, 3)
            w1t_split(0)
            quant_product(0, 3)
            link(quant_product(0, 2))
            quant_last(3).then_inc(v_q, 1)
            link(quant_last(2))
            link(TT(w1q[:, 2], w1q[:, 2], w1n[:, 2], ALU.add))
            w1t_split(1)
            by_group = w1q[:, 2].rearrange("p (g n) -> p g n", g=KC)
            link(TT(by_group, by_group, scale[:, 2 * KC:3 * KC].unsqueeze(2).to_broadcast([P, KC, P]), ALU.mult))
            TT(w1q[:, 2], w1q[:, 2], delta[:, 2], ALU.add).then_inc(v_w, 1)
            for c in range(KC):
                add_result(s_l0, 1, c, 4 + c).then_inc(v_y, 1)
            w1t_split(2)
            w1t_split(3)
            for c in range(KC):
                y_lo_of(3, 1, c)

            def split_wgu(q, s):
                dve.wait_ge(a_wg, 2 * q + s + 1)
                lo_of(wgu_lo[:, s].rearrange("p u c f -> p (u c f)"), wgu[:, s].rearrange("p u c f -> p (u c f)"),
                      wgu_hi[:, s].rearrange("p u c f -> p (u c f)")).then_inc(v_wg, 1)
                dve.wait_ge(a_bl, 2 * q + s + 1)
                whole = bl[:, s].rearrange("p a u f -> p (a u f)")
                nc.vector.scalar_tensor_tensor(whole, whole.bitcast(F32), minus_b_lo,
                                               blr[:, s].rearrange("p a u f -> p (a u f)"),
                                               ALU.mult, ALU.add).then_inc(v_bl, 1)

            def split_wd(q, s):
                dve.wait_ge(a_wd, 2 * q + s + 1)
                lo_of(wd_lo[:, s], wd[:, s], wd_hi[:, s]).then_inc(v_wd, 1)

            def split_ad(q, s, j, h):
                dve.wait_ge(p_ad, 2 * q + s + 1)
                TT(ad[:, s, :, 1], ad_raw(j, h), ad[:, s, :, 0].bitcast(F32), ALU.subtract).then_inc(v_ad, 1)

            def act_up(q, s):
                n = 2 * q + s
                dve.wait_ge(s_u, n + 1)
                dve.wait_ge(a_silu, n + 1)
                if not (isinstance(q, int) and q == 0):
                    dve.wait_ge(a_ah, n - 1)
                    dve.wait_ge(v_al, n - 1)
                TT(act[:, s], silu_g[:, s], ps[:, UP], ALU.mult).then_inc(v_act, 1)

            def act_split(q, s):
                dve.wait_ge(a_ah, 2 * q + s + 1)
                dve.wait_ge(v_act, 2 * q + s + 1)
                lo_of(act_lo[:, s], act[:, s], act_hi[:, s]).then_inc(v_al, 1)

            def ranks_up(h):
                dve.wait_ge(s_ta, h + 1)
                TT(tm[:], ps[:, SPARE], up_mask, ALU.mult).then_inc(v_tm, 1)
                dve.wait_ge(a_th, h + 1)
                lo_of(t_lo[:], tm[:], t_hi[:]).then_inc(v_tl, 1)

            def ranks_stacked(k, done, count_, bank, factor):
                dve.wait_ge(done, count_)
                nc.vector.scalar_tensor_tensor(tm[:], ps[:, bank], factor, pair_mask, ALU.mult, ALU.mult).then_inc(v_tm, 1)
                dve.wait_ge(a_th, k)
                nc.vector.scalar_tensor_tensor(td[:], t_hi[:].bitcast(F32), minus_t_lo, tm[:],
                                               ALU.mult, ALU.add).then_inc(v_tl, 1)

            for c in range(KC - 1):
                add_result(s_l1, 0, c, c).then_inc(v_y, 1)
            split_wgu(0, 0)
            add_result(s_l1, 0, KC - 1, KC - 1).then_inc(v_y, 1)
            for c in range(KC):
                y_lo_of(4, 0, c)
            add_result(s_l1, 1, 0, 4).then_inc(v_y, 1)
            dve.wait_ge(ld_masks, 16)
            ranks_up(0)
            add_result(s_l1, 1, 1, 5).then_inc(v_y, 1)
            split_wgu(0, 1)
            add_result(s_l1, 1, 2, 6).then_inc(v_y, 1)
            add_result(s_l1, 1, 3, 7).then_inc(v_y, 1)
            for c in range(KC):
                y_lo_of(5, 1, c)

            def out_result(h, c, bank):
                add_result(s_o3, h, c, bank).then_inc(v_out, 1)

            for h in range(2):
                n0 = NJ * h

                def at(j):
                    return (n0 + j) // 2, (n0 + j) % 2

                split_wd(*at(0))
                split_ad(*at(0), 0, h)
                if h == 1:
                    for c in range(KC):
                        add_result(s_dn, 0, c, DOWN + c).then_inc(v_y, 1)
                act_up(*at(0))
                if h == 1:
                    for c in range(KC):
                        y_lo_of(6, 0, c)
                act_split(*at(0))
                if h == 0:
                    dve.wait_ge(ld_t, UP_PARTS)
                    ranks_up(1)
                split_wgu(*at(2))
                split_wd(*at(1))
                split_ad(*at(1), 1, h)
                act_up(*at(1))
                act_split(*at(1))
                if h == 1:
                    ranks_stacked(4, s_t3, 1, SPARE, 2.0)
                split_wgu(*at(3))
                split_wd(*at(2))
                split_ad(*at(2), 2, h)
                if h == 1:
                    out_result(0, 0, SPARE)
                act_up(*at(2))
                if h == 1:
                    out_result(0, 1, SPARE)
                act_split(*at(2))
                if h == 1:
                    out_result(0, 2, SPARE)
                split_wgu(*at(4))
                with dve.Fori(0, 3) as i:
                    for k in range(2):
                        q, s = at(3 + k)
                        split_wd(q + i, s)
                        split_ad(q + i, s, 3 + k + 2 * i, h)
                        act_up(q + i, s)
                        act_split(q + i, s)
                        split_wgu(q + i + 1, s)
                for j in (9, 10):
                    split_wd(*at(j))
                    split_ad(*at(j), j, h)
                    act_up(*at(j))
                    act_split(*at(j))
                    if h == 0:
                        split_wgu(*at(j + 2))
                if h == 1:
                    out_result(0, 3, SPARE)
                ranks_stacked(3 + 2 * h, s_td, h + 1, TDOWN, 1.0)
            for c in range(KC):
                add_result(s_dn, 1, c, DOWN + c).then_inc(v_y, 1)
            y_lo_of(7, 1, 1)
            y_lo_of(7, 1, 3)
            ranks_stacked(6, s_t3, 2, SPARE, 2.0)
            for c in range(KC):
                out_result(1, c, (GATE, UP, TDOWN, SPARE)[c])

        @block.gpsimd
        def _(pool):
            count = [0]

            def link(ins):
                count[0] += 1
                ins.then_inc(p_chain, 1)
                pool.wait_ge(p_chain, count[0])

            TT, copy = nc.gpsimd.tensor_tensor, nc.gpsimd.tensor_copy

            def by_group(v, o):
                return v[:, KC * o:KC * (o + 1)].unsqueeze(2).to_broadcast([P, KC, P])

            def groups(v):
                return v.rearrange("p (g n) -> p g n", g=KC)

            pool.wait_ge(ld_w1, 32)
            for o in range(KC):
                pool.wait_ge(a_dc, o + 1)
                link(TT(w1n[:, o], w1[:, o], delta[:, o], ALU.add))
                if o == 0:
                    pool.wait_ge(v_rs, 1)
                TT(groups(w1n[:, o]), groups(w1n[:, o]), by_group(rscale, o), ALU.mult).then_inc(p_n, 1)

            def y_lo_of(version, h, c):
                pool.wait_ge(a_yh, KC * version + c + 1)
                TT(y_lo[:, c, half(h)], y[:, c, half(h)], y_hi[:, c, half(h)].bitcast(F32),
                   ALU.subtract).then_inc(p_yl, 1)

            def y_lo_half(version, h):
                for c in range(KC):
                    y_lo_of(version, h, c)

            y_lo_half(1, 1)
            pool.wait_ge(a_b0, 1)
            TT(b0_lo[:], b0[:], b0_hi[:].bitcast(F32), ALU.subtract).then_inc(p_b0, 1)
            pool.wait_ge(p_n, KC)
            for o in (0, 1, 3):
                if o == 3:
                    y_lo_half(2, 0)
                pool.wait_ge(v_q, min(o, 2) + 1)
                link(TT(w1q[:, o], w1q[:, o], w1n[:, o], ALU.add))
                link(TT(groups(w1q[:, o]), groups(w1q[:, o]), by_group(scale, o), ALU.mult))
                TT(w1q[:, o], w1q[:, o], delta[:, o], ALU.add).then_inc(p_w, 1)

            def split(pairs, done):
                for hi, lo, raw in pairs:
                    last = copy(hi, raw)
                link(last)
                for hi, lo, raw in pairs:
                    last = TT(lo, raw, hi.bitcast(F32), ALU.subtract)
                last.then_inc(done, 1)

            def split_ag(h):
                pool.wait_ge(ld_ag, 16 * NB)
                split([(ag[:, b // 2, :, :, b % 2, 0], ag[:, b // 2, :, :, b % 2, 1], agr[:, b])
                       for b in range(HB * h, HB * (h + 1))], p_ag)

            def split_b3(h):
                for b in range(HB * h, HB * (h + 1)):
                    raw = b3r[:, b]
                    for g in (2, 3):
                        copy(b3[:, :, b, g], raw)
                    link(copy(b3[:, :, b, 0], raw))
                    last = TT(b3[:, :, b, 1], raw, b3[:, :, b, 0].bitcast(F32), ALU.subtract)
                last.then_inc(p_b3, 1)

            def stack_b(h, p, dst, raw, ld, done):
                pool.wait_ge(ld, 16 * HB * (h + 1))
                out = dst[:, 2 * h + p]
                link(copy(out, raw[:, p]))
                link(nc.gpsimd.tensor_scalar(b_part[:], out.bitcast(F32), minus_b_lo, None, ALU.mult))
                TT(out, raw[:, p], b_part[:], ALU.add).then_inc(done, 1)
                pool.wait_ge(done, 2 * h + p + 1)

            def split_ad(q, s, j, h):
                pool.wait_ge(ld_ad, 16 * NB)
                if not (isinstance(q, int) and q == 0):
                    pool.wait_ge(s_d, 2 * q + s - 1)
                copy(ad[:, s, :, 0], ad_raw(j, h))
                copy(ad[:, s, :, 2], ad_raw(j, h))
                copy(ad[:, s, :, 3], ad_raw(j, h)).then_inc(p_ad, 1)

            split_ag(0)
            split_ag(1)
            pool.wait_ge(s_w1t, KC)
            for h in range(2):
                n0 = NJ * h

                def at(j):
                    return (n0 + j) // 2, (n0 + j) % 2

                split_ad(*at(0), 0, h)
                split_ad(*at(1), 1, h)
                if h == 0:
                    stack_b(0, 0, bd, bdr, ld_bd, p_bd)
                    stack_b(0, 1, bd, bdr, ld_bd, p_bd)
                split_ad(*at(2), 2, h)
                if h == 0:
                    stack_b(0, 0, a3, a3r, ld_a3, p_a3)
                    stack_b(0, 1, a3, a3r, ld_a3, p_a3)
                split_ad(*at(3), 3, h)
                if h == 0:
                    pool.wait_ge(ld_b3, 16 * NB)
                    pool.wait_ge(s_l0, 2 * KC)
                    split_b3(0)
                split_ad(*at(4), 4, h)
                if h == 0:
                    split_b3(1)
                with pool.Fori(1, 3) as i:
                    for k in range(2):
                        q, s = at(3 + k)
                        split_ad(q + i, s, 3 + k + 2 * i, h)
                split_ad(*at(9), 9, h)
                split_ad(*at(10), 10, h)
            for p in range(2):
                stack_b(1, p, bd, bdr, ld_bd, p_bd)
                stack_b(1, p, a3, a3r, ld_a3, p_a3)
            y_lo_of(7, 1, 0)
            y_lo_of(7, 1, 2)


def kernel(**inputs):
    import numpy as np
    import concourse.bacc as bacc
    from concourse import mybir as mb
    from concourse.bass_utils import run_bass_kernel_spmd as run

    a = {k: np.asarray(v) for k, v in inputs.items()}

    def pad_f(m, axis):
        width = [(0, 0)] * m.ndim
        width[axis] = (0, FP - F)
        return np.pad(m, width)

    def gate_up(wg, wu):
        w = np.stack([pad_f(wg, 0), pad_f(wu, 0)])
        return w.reshape(2, NJ, P, KC, P).transpose(1, 4, 0, 3, 2).reshape(NJ, P, 2 * KC * P)

    row, col = np.arange(P)[:, None], np.arange(H)[None]
    consts = np.concatenate([
        np.eye(P), np.arange(E) + 0 * row, E - np.arange(E) + 0 * row, -1.0 * (row // R % G4 == 2),
        -1.0 * (row // R % G4 == 3), 0.5 * (row // (2 * R) % 2 == col // BT % 2),
        0.5 * (row // (G4 * R) == col // BT % 2)], axis=1).astype(np.float32)
    na = a["L2_cond_A_gate"].shape[1]
    ag = np.stack([a["L2_cond_A_gate"][0], a["L2_cond_A_up"][0]])
    bg = np.stack([pad_f(a["L2_cond_B_gate"][0], 1), pad_f(a["L2_cond_B_up"][0], 1)])
    adn = pad_f(a["L2_cond_A_down"][0], 2)
    arrays = {
        "x": a["x"].reshape(TOK, D).T,
        "aw": np.concatenate([a["L0_cond_A"].reshape(E * R, D), a["L0_cond_Wr"]]).T,
        "w0": a["L0_cond_W"].T,
        "b0": a["L0_cond_B"].transpose(0, 2, 1).reshape(E * R, D),
        "w1": a["L1_cond_weight"],
        "slog": a["L1_cond_scale_log"].reshape(D, KC),
        "la1": a["L1_cond_lora_A"],
        "lb1": a["L1_cond_lora_B"].T,
        "cb": a["condB_codebook"],
        "lang": a["itok_B_0_7"],
        "idx2": a["itok_B_2_6"].reshape(1, NB),
        "idx3": a["itok_B_3_7"].reshape(1, NB),
        "wgu": gate_up(a["L2_cond_W_gate"], a["L2_cond_W_up"]),
        "wd": pad_f(a["L2_cond_W_down"], 1).T.reshape(NJ, P, D),
        "agu": ag.reshape(2, na, R, KC, P).transpose(1, 4, 3, 0, 2).reshape(na, P, KC * 2 * R),
        "bgu": bg.reshape(2, na, NJ, P, R).transpose(1, 2, 4, 0, 3).reshape(na, NJ, R, 2 * P),
        "ad": adn.reshape(na, R, NJ, P).transpose(0, 3, 2, 1).reshape(na, P, NJ * R),
        "bd": a["L2_cond_B_down"][0].transpose(0, 2, 1),
        "a3": a["L3_cond_A"].transpose(0, 2, 1),
        "b3": a["L3_cond_B"].reshape(-1, R, KC, P).transpose(0, 3, 2, 1).reshape(-1, P, KC * R),
        "consts": consts,
    }
    nc = bacc.Bacc("TRN2", target_bir_lowering=False, num_devices=1)
    feeds, aps = {}, {}
    for name, v in arrays.items():
        v = np.ascontiguousarray(v)
        feeds[name + "_dram"] = v
        aps[name] = nc.dram_tensor(name + "_dram", v.shape, mb.dt.from_np(v.dtype), kind="ExternalInput").ap()
    aps["out"] = nc.dram_tensor("out_dram", (D, TOK), mb.dt.float32, kind="ExternalOutput").ap()
    program(nc, aps)
    r = run(nc, [feeds], core_ids=[0])
    return np.ascontiguousarray(r.results[0]["out_dram"].T).reshape(NB, BT, D)
```

```python
from contextlib import ExitStack

import concourse.bass as bass
from concourse import mybir

ALU = mybir.AluOpType
ACT = mybir.ActivationFunctionType
AX_X = mybir.AxisListType.X
F32 = mybir.dt.float32
F32R = mybir.dt.float32r
BF16 = mybir.dt.bfloat16
I32 = mybir.dt.int32

P = 128
D = 512
KC = D // P
NB = 8
BT = 128
TOK = NB * BT
H = TOK // 2
HB = NB // 2
E = 8
R = 16
R1 = 64
NCB = 8
F = 1376
NJ = -(-F // P)
FP = NJ * P
AW = E * R + E
G4 = 4
STACKED = 2 * G4 * R
STACK_PARTS = 16 * 6

GATE, UP, TDOWN, SPARE, DOWN = 0, 1, 2, 3, 4


def program(nc, t):
    with ExitStack() as ctx:
        cursor = [-(-nc.sbuf_base // 64) * 64]

        def sb(name, shape, dt=F32, at=None):
            n = 4
            for s in shape[1:]:
                n *= s
            off = cursor[0] if at is None else at
            if at is None:
                cursor[0] += -(-n // 64) * 64
            return nc.alloc_sbuf_tensor_at(name, list(shape), dt, offset=off)

        def sem(name):
            return ctx.enter_context(nc.semaphore(name))

        ps = ctx.enter_context(nc.psum_tensor("ps", [P, 8, 512], F32))

        y = sb("y", [P, KC, TOK])
        y_hi = sb("y_hi", [P, KC, TOK], F32R)
        y_lo = sb("y_lo", [P, KC, TOK], F32R)

        aw = sb("aw", [P, KC, AW])
        consts = sb("consts", [P, P + 2 * H + 2 * E + 2])
        ident = consts[:, 0:P]
        e_iota = consts[:, P:P + E]
        e_rank = consts[:, P + E:P + 2 * E]
        minus_b_lo = consts[:, P + 2 * E:P + 2 * E + 1]
        minus_t_lo = consts[:, P + 2 * E + 1:P + 2 * E + 2]
        masks = P + 2 * E + 2
        up_mask = consts[:, masks:masks + H]
        pair_mask = consts[:, masks + H:masks + 2 * H]
        lang_i = sb("lang_i", [P, NB], I32)
        lang_f = sb("lang_f", [P, NB])
        bias = sb("bias", [P, NB, E])
        rt = sb("rt", [P, 6, NB, E])
        rs1 = sb("rs1", [P, 8, NB])
        gates = sb("gates", [P, NB, E])
        gated = sb("gated", [P, NB, E, R])
        gh_hi = sb("gh_hi", [P, TOK], F32R)
        gh_lo = sb("gh_lo", [P, TOK], F32R)
        early = cursor[0]
        lora1 = sb("lora1", [R1, 2, D])
        b0 = sb("b0", [P, D])
        b0_hi = sb("b0_hi", [P, D], F32R)
        b0_lo = sb("b0_lo", [P, D], F32R)
        slog = sb("slog", [P, KC * KC])
        scale = sb("scale", [P, KC * KC])
        rscale = sb("rscale", [P, KC * KC])
        cbk = sb("cbk", [P, NCB])
        cbt = sb("cbt", [P, 6, NCB])

        c_abs, c_n, thr, u, step = (cbt[:, k] for k in range(5))

        region = cursor[0]
        w0 = sb("w0", [P, KC, D])
        w0_hi = sb("w0_hi", [P, KC, D], F32R)
        w0_lo = sb("w0_lo", [P, KC, D], F32R)
        w1q = sb("w1q", [P, KC, D])
        region2 = cursor[0]
        w1 = sb("w1", [P, KC, D])
        delta = sb("delta", [P, KC, D])
        w1n = sb("w1n", [P, KC, D])
        w1t_hi = sb("w1t_hi", [P, KC, KC, P], F32R, at=region2 + 2 * KC * D * 4)
        lora1_hi = sb("lora1_hi", [R1, 2, D], F32R, at=cursor[0])
        lora1_lo = sb("lora1_lo", [R1, 2, D], F32R, at=cursor[0] + 2 * D * 4)
        w1t_lo = sb("w1t_lo", [P, KC, KC, P], F32R)

        KB = 1024
        wgu_hi = sb("wgu_hi", [P, 2, 2, KC, P], F32R, at=region)
        wgu_lo = sb("wgu_lo", [P, 2, 2, KC, P], F32R, at=region + 8 * KB)
        wd_hi = sb("wd_hi", [P, 2, D], F32R, at=region + 16 * KB)
        wd_lo = sb("wd_lo", [P, 2, D], F32R, at=region + 20 * KB)
        bl = sb("bl", [P, 2, 2, 2, P], F32R, at=region + 24 * KB)
        ad = sb("ad", [P, 2, HB, G4, R], F32R, at=region + 28 * KB)
        dn_hi = sb("dn_hi", [P, KC, H], F32R, at=region)
        dn_lo = sb("dn_lo", [P, KC, H], F32R, at=region + 8 * KB)
        act_hi = sb("act_hi", [P, 2, H], F32R, at=region2 + 16 * KB)
        act_lo = sb("act_lo", [P, 2, H], F32R, at=region2 + 20 * KB)
        act = sb("act", [P, 2, H], at=region2 + 24 * KB)
        silu_g = sb("silu_g", [P, 2, H], at=region2 + 28 * KB)
        tg = sb("tg", [P, 2, H], F32R, at=region2)
        tu = sb("tu", [P, 2, H], F32R, at=region2 + 4 * KB)
        td = sb("td", [P, H], F32R, at=region2 + 8 * KB)
        tm = sb("tm", [P, H], at=region2 + 10 * KB)
        t_hi = sb("t_hi", [P, H], F32R, at=region2 + 12 * KB)
        t_lo = sb("t_lo", [P, H], F32R, at=region2 + 14 * KB)

        wgu = sb("wgu", [P, 2, 2, KC, P])
        wd = sb("wd", [P, 2, D])
        blr = sb("blr", [P, 2, 2, 2, P])
        agr = sb("agr", [P, NB, KC, 2, R])
        ag = sb("ag", [P, 4, KC, 2, 2, 2, R], F32R)
        adr = sb("adr", [P, NB, NJ, R])
        bdr = sb("bdr", [P, 2, D])
        bd = sb("bd", [P, 4, D], F32R)
        a3r = sb("a3r", [P, 2, D])
        a3 = sb("a3", [P, 4, D], F32R)
        b3r = sb("b3r", [P, NB, KC, R])
        b_part = sb("b_part", [P, D])
        b3 = sb("b3", [P, KC, NB, G4, R], F32R, at=early)
        idx = sb("idx", [1, 2 * NB], I32)
        ident_r = sb("ident_r", [P, P], F32R)
        idle = sb("idle", [P, 512], BF16)
        assert cursor[0] <= nc.sbuf_usable_end

        ld_aw, ld_l1, ld_c, ld_masks, ld_cb, ld_slog, ld_lang, ld_w1, ld_w0, ld_b0, ld_idx = (
            sem(n) for n in ("ld_aw", "ld_l1", "ld_c", "ld_masks", "ld_cb", "ld_slog", "ld_lang", "ld_w1", "ld_w0", "ld_b0", "ld_idx"))
        ld_x = [sem("ld_x0"), sem("ld_x1")]
        ld_ag, ld_ad, ld_b3 = sem("ld_ag"), sem("ld_ad"), sem("ld_b3")
        ld_bd, ld_a3 = sem("ld_bd"), sem("ld_a3")
        ld_wgu = [sem("ld_wgu0"), sem("ld_wgu1")]
        ld_wd = [sem("ld_wd0"), sem("ld_wd1")]
        ld_bl = [sem("ld_bl0"), sem("ld_bl1")]
        ld_t, st_out = [sem("ld_tg"), sem("ld_tu")], sem("st_out")
        s_delta, s_hlog, s_l0, s_ght, s_w1t, s_l1 = (
            sem(n) for n in ("s_delta", "s_hlog", "s_l0", "s_ght", "s_w1t", "s_l1"))
        s_ta, s_g, s_u, s_d, s_td, s_dn, s_t3, s_o3 = (
            sem(n) for n in ("s_ta", "s_g", "s_u", "s_d", "s_td", "s_dn", "s_t3", "s_o3"))
        a_dc, a_es, a_exp, a_yh, a_w0, a_b0, a_gh, a_w1t = (
            sem(n) for n in ("a_dc", "a_es", "a_exp", "a_yh", "a_w0", "a_b0", "a_gh", "a_w1t"))
        a_th, a_silu, a_ah, a_wg, a_wd, a_bl = (sem(n) for n in ("a_th", "a_silu", "a_ah", "a_wg", "a_wd", "a_bl"))
        v_chain, v_rs, v_dc, v_dm, v_gate, v_y, v_yl, v_w0, v_gh, v_q, v_w1t = (
            sem(n) for n in ("v_chain", "v_rs", "v_dc", "v_dm", "v_gate", "v_y", "v_yl", "v_w0",
                             "v_gh", "v_q", "v_w1t"))
        v_step, a_step, p_yl, p_b0, v_w, v_idle, a_l1, v_l1, a_ident, a_dn, v_dn, a_out, p_step = (sem(n) for n in ("v_step", "a_step", "p_yl", "p_b0", "v_w", "v_idle", "a_l1", "v_l1",
                                                      "a_ident", "a_dn", "v_dn", "a_out", "p_step"))
        v_tm, v_tl, v_act, v_al, v_wg, v_wd, v_ad, v_bl, v_out = (
            sem(n) for n in ("v_tm", "v_tl", "v_act", "v_al", "v_wg", "v_wd", "v_ad", "v_bl", "v_out"))
        p_chain, p_n, p_w, p_ag, p_ad, p_bd, p_a3, p_b3 = (
            sem(n) for n in ("p_chain", "p_n", "p_w", "p_ag", "p_ad", "p_bd", "p_a3", "p_b3"))

        def by_group(v, o):
            return v[:, KC * o:KC * (o + 1)].unsqueeze(2).to_broadcast([P, KC, P])

        def groups(v):
            return v.rearrange("p (g n) -> p g n", g=KC)

        def half(h):
            return slice(h * H, (h + 1) * H)

        y_lo_by = {0: (v_yl, KC), 1: (p_yl, KC), 2: (p_yl, 2 * KC), 3: (p_yl, 3 * KC)}
        y_lo_by.update({v: (v_yl, KC * (v - 2)) for v in range(4, 7)})

        w1_by = ((p_w, 1), (p_w, 2), (v_w, 1), (p_w, 3))

        quant_order = [(k, o) for pair in ((0, 1), (2, 3)) for k in range(6, 0, -1) for o in pair]
        products = [e for e in quant_order if e not in ((6, 2), (6, 3))]

        def ad_raw(j, h):
            return adr[:, HB * h:HB * (h + 1), bass.ds(j, 1), :].rearrange("p b j r -> p b (j r)")

        block = ctx.enter_context(nc.Block())

        @block.sync
        def _(sp):
            def chunks(ap):
                return ap.rearrange("(c p) n -> p c n", p=P)

            xv, w1v, w0v = chunks(t["x"]), chunks(t["w1"]), chunks(t["w0"])

            def load_x(h):
                for c in range(0, KC, 2):
                    sp.dma_start(y[:, c:c + 2, half(h)], xv[:, c:c + 2, half(h)]).then_inc(ld_x[h], 16)

            sp.dma_start(lora1[:], t["lora1"].rearrange("r (u n) -> r u n", u=2)).then_inc(ld_l1, 16)
            sp.dma_start(cbk[:], t["cb"].partition_broadcast(P)).then_inc(ld_cb, 16)
            sp.dma_start(slog[:].rearrange("p (c g) -> p c g", g=KC), chunks(t["slog"])).then_inc(ld_slog, 16)
            sp.dma_start(aw[:], chunks(t["aw"])).then_inc(ld_aw, 16)
            sp.dma_start(lang_i[:], t["lang"].partition_broadcast(P)).then_inc(ld_lang, 16)
            sp.dma_start(consts[:, 0:masks], t["consts"][:, 0:masks]).then_inc(ld_c, 16)
            load_x(0)
            for c in range(0, KC, 2):
                sp.dma_start(w0[:, c:c + 2], w0v[:, c:c + 2]).then_inc(ld_w0, 16)
            for c in range(0, KC, 2):
                sp.dma_start(w1[:, c:c + 2], w1v[:, c:c + 2]).then_inc(ld_w1, 16)
            load_x(1)
            sp.dma_start(b0[:], t["b0"]).then_inc(ld_b0, 16)
            sp.dma_start(idx[:, 0:NB], t["idx2"]).then_inc(ld_idx, 16)
            sp.dma_start(idx[:, NB:2 * NB], t["idx3"]).then_inc(ld_idx, 16)
            sp.dma_start(consts[:, masks:], t["consts"][:, masks:]).then_inc(ld_masks, 16)
            sp.wait_ge(ld_idx, 32)

            def adapter2(b):
                return sp.value_load(idx[0:1, b:b + 1], min_val=0, max_val=15)

            def adapter3(b):
                return sp.value_load(idx[0:1, NB + b:NB + b + 1], min_val=0, max_val=7)

            def grouped(tile_ap, b2):
                return tile_ap[b2 * G4 * R:(b2 + 1) * G4 * R]

            def repeated(ap):
                r, n = ap.shape
                return ap.unsqueeze(0).to_broadcast([G4, r, n])

            def load_a(b):
                sp.dma_start(agr[:, b], t["agu"][bass.ds(adapter2(b), 1)].rearrange("a p n -> (a p) n")).then_inc(ld_ag, 16)

            def load_ad(b):
                sp.dma_start(adr[:, b], t["ad"][bass.ds(adapter2(b), 1)].rearrange("a p n -> (a p) n")).then_inc(ld_ad, 16)

            def load_b3(b):
                i3 = adapter3(b)
                sp.dma_start(b3r[:, b], t["b3"][bass.ds(i3, 1)].rearrange("a p n -> (a p) n")).then_inc(ld_b3, 16)

            def load_bd_a3(h):
                if h == 1:
                    sp.wait_ge(p_bd, 2)
                    sp.wait_ge(p_a3, 2)
                for b in range(HB):
                    i2 = adapter2(HB * h + b)
                    i3 = adapter3(HB * h + b)
                    sp.dma_start(grouped(bdr[:, b // 2], b % 2),
                                 repeated(t["bd"][bass.ds(i2, 1)].rearrange("a r n -> (a r) n"))).then_inc(ld_bd, 16)
                    sp.dma_start(grouped(a3r[:, b // 2], b % 2),
                                 repeated(t["a3"][bass.ds(i3, 1)].rearrange("a r n -> (a r) n"))).then_inc(ld_a3, 16)

            def load_wgu(j, q, s, h):
                if not (isinstance(q, int) and q == 0):
                    sp.wait_ge(a_wg, 2 * q + s - 1)
                    sp.wait_ge(v_wg, 2 * q + s - 1)
                    sp.wait_ge(v_bl, 2 * q + s - 1)
                sp.dma_start(wgu[:, s], t["wgu"][bass.ds(j, 1)].rearrange("j p n -> (j p) n")).then_inc(ld_wgu[s], 16)
                for b in range(HB):
                    src = t["bgu"][bass.ds(bl_idx[HB * h + b], 1), bass.ds(j, 1)].rearrange("a j r n -> (a j r) n")
                    sp.dma_start(grouped(blr[:, s, b // 2].rearrange("p u f -> p (u f)"), b % 2),
                                 repeated(src)).then_inc(ld_bl[s], 16)

            def load_wd(j, q, s):
                if not (isinstance(q, int) and q == 0):
                    sp.wait_ge(a_wd, 2 * q + s - 1)
                    sp.wait_ge(v_wd, 2 * q + s - 1)
                sp.dma_start(wd[:, s], t["wd"][bass.ds(j, 1)].rearrange("j p n -> (j p) n")).then_inc(ld_wd[s], 16)

            def stack_up(h):
                sp.wait_ge(a_th, h + 1)
                sp.wait_ge(v_tl, h + 1)
                for u, dst in enumerate((tg, tu)):
                    for b in range(2):
                        to, row = b * G4 * R, (u * 2 + b) * 2 * R
                        for src, rows, at_ in ((t_hi, 2 * R, 0), (t_hi, R, 2 * R), (t_lo, R, 3 * R)):
                            sp.dma_start(dst[to + at_:to + at_ + rows, h].bitcast(F32),
                                            src[row:row + rows].bitcast(F32)).then_inc(ld_t[u], 16)

            bl_idx = {b: adapter2(b) for b in range(HB)}
            load_wgu(0, 0, 0, 0)
            load_wgu(1, 0, 1, 0)
            for b in range(NB):
                load_a(b)
            load_wd(0, 0, 0)
            for b in range(NB):
                load_ad(b)
            load_bd_a3(0)
            for b in range(NB):
                load_b3(b)
            for h in range(2):
                n0 = NJ * h
                if h == 1:
                    load_wd(0, n0 // 2, n0 % 2)
                if h == 1:
                    load_wgu(2, (n0 + 2) // 2, n0 % 2, h)
                for j in (1, 2):
                    n = n0 + j
                    load_wd(j, n // 2, n % 2)
                    if h == 0:
                        stack_up(j - 1)
                    if h == 0 and j == 1:
                        load_wgu(2, (n0 + 2) // 2, n0 % 2, h)
                    load_wgu(j + 2, (n + 2) // 2, n % 2, h)
                if h == 1:
                    load_bd_a3(1)
                with sp.Fori(0, 3) as i:
                    for k in range(2):
                        n = n0 + 3 + k
                        load_wd(3 + k + 2 * i, n // 2 + i, n % 2)
                        load_wgu(5 + k + 2 * i, (n + 2) // 2 + i, n % 2, h)
                if h == 0:
                    bl_idx.update({b: adapter2(b) for b in range(HB, NB)})
                for j in (9, 10):
                    n = n0 + j
                    load_wd(j, n // 2, n % 2)
                    if h == 0:
                        load_wgu(j - 9, (n + 2) // 2, n % 2, 1)
            ov = t["out"].rearrange("(c p) n -> p c n", p=P)
            for h in range(2):
                for c in (range(KC) if h == 0 else (0, 1, 3)):
                    if h == 1 and c == 0:
                        sp.wait_ge(a_out, 1)
                    else:
                        sp.wait_ge(v_out, c + 1 if h == 0 else KC + c // 2 + 1)
                    sp.dma_start(ov[:, c, half(h)], y[:, c, half(h)]).then_inc(st_out, 16)
            sp.wait_ge(st_out, 16 * 2 * KC)

        @block.tensor
        def _(pe):
            def three(out, w_hi, w_lo, r_hi, r_lo, start, stop):
                nc.tensor.matmul(out, w_hi, r_hi, start=start, stop=False, skip_group_check=True)
                nc.tensor.matmul(out, w_hi, r_lo, start=False, stop=False, skip_group_check=True)
                return nc.tensor.matmul(out, w_lo, r_hi, start=False, stop=stop, skip_group_check=True)

            def y_ready(group):
                pe.wait_ge(a_yh, KC * (group + 1))
                pe.wait_ge(*y_lo_by[group])

            def keep_warm(bank, n):
                for _ in range(n):
                    nc.tensor.matmul(ps[:, bank], idle[:, 0:P], idle[:], start=True, stop=True)

            pe.wait_ge(v_idle, 1)
            keep_warm(7, 11)
            pe.wait_ge(a_l1, 1)
            pe.wait_ge(v_l1, 1)
            for o in range(KC):
                three(ps[:, o], lora1_hi[:, 0, o * P:(o + 1) * P], lora1_lo[:, 0, o * P:(o + 1) * P],
                      lora1_hi[:, 1], lora1_lo[:, 1], True, True).then_inc(s_delta, 1)

            def router(h):
                pe.wait_ge(ld_x[h], 32)
                for b in range(HB * h, HB * (h + 1)):
                    out = ps[:, 4 + b // 2, (b % 2) * AW:(b % 2 + 1) * AW]
                    for c in range(KC):
                        last = nc.tensor.matmul(out, y[:, c, b * BT:(b + 1) * BT], aw[:, c],
                                                start=(c == 0), stop=(c == KC - 1))
                    if b % 2:
                        last.then_inc(s_hlog, 1)

            pe.wait_ge(ld_aw, 16)
            router(0)

            def l0_base(h, o):
                for c in range(KC):
                    if h == 0 and o == 0:
                        pe.wait_ge(a_w0, c + 1)
                        pe.wait_ge(v_w0, c + 1)
                    three(ps[:, 4 * h + o], w0_hi[:, c, o * P:(o + 1) * P], w0_lo[:, c, o * P:(o + 1) * P],
                          y_hi[:, c, half(h)], y_lo[:, c, half(h)], c == 0, False)

            def l0_lora(h):
                pe.wait_ge(a_b0, 1)
                pe.wait_ge(p_b0, 1)
                pe.wait_ge(a_gh, h + 1)
                pe.wait_ge(v_gh, h + 1)
                for o in range(KC):
                    three(ps[:, 4 * h + o], b0_hi[:, o * P:(o + 1) * P], b0_lo[:, o * P:(o + 1) * P],
                          gh_hi[:, half(h)], gh_lo[:, half(h)], False, True).then_inc(s_l0, 1)

            y_ready(0)
            pe.wait_ge(a_dc, 2)
            pe.wait_ge(v_dc, 2)
            l0_base(0, 0)
            router(1)
            for o in range(1, KC):
                l0_base(0, o)
            pe.wait_ge(ld_c, 16)
            pe.wait_ge(v_gate, 1)
            for b in range(NB):
                last = nc.tensor.transpose(ps[:, 4 + b // HB, b % HB * BT:(b % HB + 1) * BT],
                                           gated[:, b].rearrange("p e r -> p (e r)"), ident)
                if b % HB == HB - 1:
                    last.then_inc(s_ght, 1)
            y_ready(1)
            l0_base(1, 2)
            l0_lora(0)
            l0_base(1, 3)
            pe.wait_ge(a_gh, 2)
            pe.wait_ge(v_gh, 2)
            l0_base(1, 0)

            def w1_transpose(o):
                pe.wait_ge(v_y, o + 1)
                pe.wait_ge(*w1_by[o])
                for c in range(KC):
                    last = nc.tensor.transpose(ps[:, o, c * P:(c + 1) * P], w1q[:, o, c * P:(c + 1) * P], ident)
                last.then_inc(s_w1t, 1)

            w1_transpose(0)
            l0_base(1, 1)
            w1_transpose(1)
            l0_lora(1)

            def l1(h, o):
                pe.wait_ge(a_w1t, o + 1)
                pe.wait_ge(v_w1t, o + 1)
                for c in range(KC):
                    last = three(ps[:, 4 * h + o], w1t_hi[:, o, c], w1t_lo[:, o, c],
                                 y_hi[:, c, half(h)], y_lo[:, c, half(h)], c == 0, c == KC - 1)
                last.then_inc(s_l1, 1)

            def t_up(h):
                pe.wait_ge(p_ag, h + 1)
                if h == 0:
                    pe.wait_ge(v_y, KC * 3)
                lo_by, lo_count = y_lo_by[4 + h]
                for c in range(KC):
                    for part, y_part in enumerate((y_hi, y_lo)):
                        if part == 0:
                            pe.wait_ge(a_yh, KC * (4 + h) + c + 1)
                        else:
                            pe.wait_ge(lo_by, lo_count - KC + c + 1)
                        for p in range(2):
                            w = ag[:, 2 * h + p, c].rearrange("p u b s r -> p (u b s r)")
                            cols = slice(h * H + p * 2 * BT, h * H + (p + 1) * 2 * BT)
                            last = nc.tensor.matmul(ps[:, SPARE, p * 2 * BT:(p + 1) * 2 * BT], w, y_part[:, c, cols],
                                                    start=(c == 0 and part == 0 and p == 0), stop=(c == KC - 1 and part == 1),
                                                    skip_group_check=True)
                last.then_inc(s_ta, 1)

            y_ready(2)
            l1(0, 0)
            l1(0, 1)
            w1_transpose(2)
            w1_transpose(3)
            l1(0, 2)
            l1(0, 3)
            y_ready(3)
            l1(1, 0)
            t_up(0)
            l1(1, 1)
            l1(1, 2)
            l1(1, 3)

            def gate_or_up(which, bank, s, h, done):
                for c in range(KC):
                    three(ps[:, bank], wgu_hi[:, s, which, c], wgu_lo[:, s, which, c],
                          y_hi[:, c, half(h)], y_lo[:, c, half(h)], c == 0, False)
                pe.wait_ge(ld_t[which], STACK_PARTS * (h + 1))
                tt = tg if which == 0 else tu
                for p in range(2):
                    last = nc.tensor.matmul(ps[:, bank, p * 2 * BT:(p + 1) * 2 * BT], bl[:, s, p, which],
                                            tt[:, h, p * 2 * BT:(p + 1) * 2 * BT], start=False, stop=(p == 1),
                                            skip_group_check=True)
                last.then_inc(done, 1)

            def gate(q, s, h, first=False):
                n = 2 * q + s
                pe.wait_ge(a_wg, n + 1)
                pe.wait_ge(v_wg, n + 1)
                pe.wait_ge(v_bl, n + 1)
                if not first:
                    pe.wait_ge(a_silu, n)
                gate_or_up(0, GATE, s, h, s_g)

            def up(q, s, h, first=False):
                if not first:
                    pe.wait_ge(v_act, 2 * q + s)
                gate_or_up(1, UP, s, h, s_u)

            def t_down(q, s, first):
                n = 2 * q + s
                pe.wait_ge(a_ah, n + 1)
                pe.wait_ge(v_al, n + 1)
                pe.wait_ge(p_ad, n + 1)
                pe.wait_ge(v_ad, n + 1)
                for p in range(2):
                    cols = slice(p * 2 * BT, (p + 1) * 2 * BT)
                    out = ps[:, TDOWN, cols]
                    w = ad[:, s, 2 * p:2 * p + 2].rearrange("p b g r -> p (b g r)")
                    nc.tensor.matmul(out, w, act_hi[:, s, cols], start=(first and p == 0), stop=False,
                                     skip_group_check=True)
                    last = nc.tensor.matmul(out, w, act_lo[:, s, cols], start=False, stop=False,
                                            skip_group_check=True)
                return last

            def down(q, s, first=False):
                n = 2 * q + s
                pe.wait_ge(a_wd, n + 1)
                pe.wait_ge(v_wd, n + 1)
                for o in range(KC):
                    last = three(ps[:, DOWN + o], wd_hi[:, s, o * P:(o + 1) * P], wd_lo[:, s, o * P:(o + 1) * P],
                                 act_hi[:, s], act_lo[:, s], first, False)
                last.then_inc(s_d, 1)

            def down_lora(h):
                pe.wait_ge(p_bd, 2 * (h + 1))
                pe.wait_ge(v_tl, 3 + 2 * h)
                for o in range(KC):
                    for p in range(2):
                        cols = slice(p * 2 * BT, (p + 1) * 2 * BT)
                        last = nc.tensor.matmul(ps[:, DOWN + o, cols], bd[:, 2 * h + p, o * P:(o + 1) * P], td[:, cols],
                                                start=False, stop=(p == 1), skip_group_check=True)
                    last.then_inc(s_dn, 1)

            def b3_product(h, c, hi, lo, start, stop):
                for part, v in enumerate((hi, lo)):
                    for p in range(2):
                        w = b3[:, c, HB * h + 2 * p:HB * h + 2 * p + 2].rearrange("p b g r -> p (b g r)")
                        last = nc.tensor.matmul(ps[:, SPARE, p * 2 * BT:(p + 1) * 2 * BT], w,
                                                v[:, p * 2 * BT:(p + 1) * 2 * BT],
                                                start=(start and part == 0 and p == 0), stop=(stop and part == 1),
                                                skip_group_check=True)
                return last

            def t_three(h):
                pe.wait_ge(p_b3, h + 1)
                y_ready(6)
                for c in range(KC):
                    last = b3_product(h, c, y_hi[:, c, half(h)], y_lo[:, c, half(h)], c == 0, c == KC - 1)
                last.then_inc(s_t3, 1)

            def last_results():
                banks = (GATE, UP, TDOWN, DOWN)

                def add(o, hi, lo, start):
                    nc.tensor.matmul(ps[:, banks[o]], ident_r[:], hi, start=start, stop=False, skip_group_check=True)
                    nc.tensor.matmul(ps[:, banks[o]], ident_r[:], lo, start=False, stop=False, skip_group_check=True)

                pe.wait_ge(p_b3, 2)
                pe.wait_ge(v_out, KC)
                for c in range(KC):
                    b3_product(1, c, y_hi[:, c, half(1)], y_lo[:, c, half(1)], c == 0, False)
                for c in range(KC):
                    pe.wait_ge(a_dn, c + 1)
                    pe.wait_ge(v_dn, c + 1)
                    last = b3_product(1, c, dn_hi[:, c], dn_lo[:, c], False, c == KC - 1)
                last.then_inc(s_t3, 1)
                pe.wait_ge(a_ident, 1)
                for o in range(KC):
                    if o % 2 == 0:
                        add(o, y_hi[:, o, half(1)], y_lo[:, o, half(1)], True)
                    add(o, dn_hi[:, o], dn_lo[:, o], o % 2 == 1)
                for o in range(KC):
                    out_three(1, o, banks[o])

            def out_three(h, o, bank):
                if h == 0 and o > 0:
                    pe.wait_ge(v_out, o)
                pe.wait_ge(p_a3, 2 * (h + 1))
                pe.wait_ge(v_tl, 4 + 2 * h)
                for p in range(2):
                    cols = slice(p * 2 * BT, (p + 1) * 2 * BT)
                    last = nc.tensor.matmul(ps[:, bank, cols], a3[:, 2 * h + p, o * P:(o + 1) * P], td[:, cols],
                                            start=(h == 0 and p == 0), stop=True, skip_group_check=True)
                last.then_inc(s_o3, 1)

            for h in range(2):
                n0 = NJ * h

                def at(j):
                    return (n0 + j) // 2, (n0 + j) % 2

                y_ready(4 + h)
                gate(*at(0), h, first=(h == 0))
                if h == 1:
                    down_lora(0)
                up(*at(0), h, first=(h == 0))
                if h == 0:
                    pe.wait_ge(v_tm, 1)
                    t_up(1)
                gate(*at(1), h)
                up(*at(1), h)
                if h == 1:
                    t_three(0)
                pe.wait_ge(v_y, KC * (4 if h == 0 else 5))
                if h == 1:
                    pe.wait_ge(v_tm, 3)
                t_down(*at(0), True)
                down(*at(0), first=True)
                gate(*at(2), h)
                if h == 1:
                    pe.wait_ge(v_tm, 4)
                    out_three(0, 0, SPARE)
                up(*at(2), h)
                if h == 1:
                    out_three(0, 1, SPARE)
                t_down(*at(1), False)
                down(*at(1))
                if h == 1:
                    out_three(0, 2, SPARE)
                with pe.Fori(0, 4) as i:
                    for k in range(2):
                        q, s = at(3 + k)
                        gate(q + i, s, h)
                        up(q + i, s, h)
                        q, s = at(2 + k)
                        t_down(q + i, s, False)
                        down(q + i, s)
                if h == 1:
                    out_three(0, 3, SPARE)
                t_down(*at(NJ - 1), False).then_inc(s_td, 1)
                down(*at(NJ - 1))
            down_lora(1)
            last_results()

        @block.scalar
        def _(act_e):
            def cast(out, in_):
                return nc.scalar.activation(out, in_, ACT.Copy)

            def split_y(h, c):
                return cast(y_hi[:, c, half(h)], y[:, c, half(h)]).then_inc(a_yh, 1)

            def result_hi(layer, h):
                if layer < 2:
                    act_e.wait_ge((s_l0, s_l1)[layer], KC * (h + 1))
                for c in range(KC):
                    act_e.wait_ge(v_y, KC * (2 * layer + h) + c + 1)
                    split_y(h, c)

            def quant_add(events):
                for k, o in events:
                    if k == 6 and o >= 2:
                        act_e.wait_ge(p_step, o - 1)
                    else:
                        act_e.wait_ge(v_step, products.index((k, o)) + 1)
                    nc.scalar.activation(w1q[:, o], w1q[:, o], ACT.Identity, bias=step[:, k - 1:k]).then_inc(a_step, 1)

            act_e.wait_ge(ld_l1, 16)
            cast(lora1_hi[:], lora1[:]).then_inc(a_l1, 1)
            act_e.wait_ge(ld_slog, 16)
            nc.scalar.activation(scale[:], slog[:], ACT.Exp).then_inc(a_es, 1)
            for o in range(2):
                act_e.wait_ge(s_delta, o + 1)
                nc.scalar.activation(delta[:, o], ps[:, o], ACT.Copy, scale=0.5).then_inc(a_dc, 1)
            act_e.wait_ge(ld_x[0], 32)
            for c in range(KC):
                split_y(0, c)
            act_e.wait_ge(ld_w0, 32)
            for c in range(KC):
                cast(w0_hi[:, c], w0[:, c]).then_inc(a_w0, 1)
            quant_add(quant_order[0:4])
            act_e.wait_ge(ld_x[1], 32)
            split_y(1, 0)
            split_y(1, 1)
            split_y(1, 2)
            split_y(1, 3)
            quant_add(quant_order[4:6])
            act_e.wait_ge(ld_b0, 16)
            cast(b0_hi[:], b0[:]).then_inc(a_b0, 1)
            act_e.wait_ge(v_dm, 1)
            nc.scalar.activation(rs1[:, 3], rs1[:, 2], ACT.Exp).then_inc(a_exp, 1)
            quant_add(quant_order[6:10])
            for h in range(2):
                act_e.wait_ge(s_ght, h + 1)
                cast(gh_hi[:, half(h)], ps[:, 4 + h]).then_inc(a_gh, 1)
                quant_add(quant_order[10 + 2 * h:12 + 2 * h])
            result_hi(0, 0)
            quant_add(quant_order[14:20])

            def w1t_split(o):
                act_e.wait_ge(s_w1t, o + 1)
                cast(w1t_hi[:, o].rearrange("p c n -> p (c n)"), ps[:, o]).then_inc(a_w1t, 1)

            w1t_split(0)
            quant_add(quant_order[20:22])
            w1t_split(1)
            quant_add(quant_order[22:])
            w1t_split(2)
            result_hi(0, 1)
            w1t_split(3)

            def split_wgu(q, s):
                n = 2 * q + s
                if not (isinstance(q, int) and q == 0):
                    act_e.wait_ge(s_u, n - 1)
                act_e.wait_ge(ld_wgu[s], 16 * (q + 1))
                cast(wgu_hi[:, s].rearrange("p u c f -> p (u c f)"),
                     wgu[:, s].rearrange("p u c f -> p (u c f)")).then_inc(a_wg, 1)
                act_e.wait_ge(ld_bl[s], 16 * HB * (q + 1))
                cast(bl[:, s].rearrange("p a u f -> p (a u f)"),
                     blr[:, s].rearrange("p a u f -> p (a u f)")).then_inc(a_bl, 1)

            def split_wd(q, s):
                n = 2 * q + s
                if not (isinstance(q, int) and q == 0):
                    act_e.wait_ge(s_d, n - 1)
                act_e.wait_ge(ld_wd[s], 16 * (q + 1))
                cast(wd_hi[:, s], wd[:, s]).then_inc(a_wd, 1)

            act_e.wait_ge(ld_c, 16)
            act_e.wait_ge(s_l0, 2 * KC)
            split_wgu(0, 0)
            result_hi(1, 0)

            def silu(q, s):
                n = 2 * q + s
                act_e.wait_ge(s_g, n + 1)
                if not (isinstance(q, int) and q == 0):
                    act_e.wait_ge(v_act, n - 1)
                nc.scalar.activation(silu_g[:, s], ps[:, GATE], ACT.Silu).then_inc(a_silu, 1)

            def act_split(q, s):
                n = 2 * q + s
                act_e.wait_ge(v_act, n + 1)
                if not (isinstance(q, int) and q == 0):
                    act_e.wait_ge(s_d, n - 1)
                cast(act_hi[:, s], act[:, s]).then_inc(a_ah, 1)

            def ranks_hi(k):
                act_e.wait_ge(v_tm, k)
                cast(t_hi[:], tm[:]).then_inc(a_th, 1)

            ranks_hi(1)
            cast(ident_r[:], ident).then_inc(a_ident, 1)
            split_wgu(0, 1)
            result_hi(1, 1)
            for h in range(2):
                n0 = NJ * h

                def at(j):
                    return (n0 + j) // 2, (n0 + j) % 2

                split_wd(*at(0))
                silu(*at(0))
                if h == 1:
                    result_hi(2, 0)
                act_split(*at(0))
                if h == 0:
                    act_e.wait_ge(ld_t[0], STACK_PARTS)
                    act_e.wait_ge(ld_t[1], STACK_PARTS)
                    ranks_hi(2)
                split_wgu(*at(2))
                split_wd(*at(1))
                silu(*at(1))
                act_split(*at(1))
                if h == 1:
                    ranks_hi(4)
                split_wgu(*at(3))
                silu(*at(2))
                split_wd(*at(2))
                act_split(*at(2))
                split_wgu(*at(4))
                with act_e.Fori(0, 3) as i:
                    for k in range(2):
                        q, s = at(3 + k)
                        split_wd(q + i, s)
                        silu(q + i, s)
                        act_split(q + i, s)
                        split_wgu(q + i + 1, s)
                for j in (9, 10):
                    split_wd(*at(j))
                    silu(*at(j))
                    act_split(*at(j))
                    if h == 0:
                        split_wgu(*at(j + 2))
                if h == 0:
                    act_e.wait_ge(ld_t[0], 2 * STACK_PARTS)
                    act_e.wait_ge(ld_t[1], 2 * STACK_PARTS)
                ranks_hi(3 + 2 * h)
            for c in range(KC):
                act_e.wait_ge(s_dn, KC + c + 1)
                cast(dn_hi[:, c], ps[:, DOWN + c]).then_inc(a_dn, 1)
            ranks_hi(6)
            for o, bank in ((0, GATE), (2, TDOWN)):
                act_e.wait_ge(s_o3, KC + o + 1)
                cast(y[:, o, half(1)], ps[:, bank]).then_inc(a_out, 1)
            act_e.wait_ge(a_out, 2)
            act_e.dma_start(t["out"].rearrange("(c p) n -> p c n", p=P)[:, 2, half(1)],
                            y[:, 2, half(1)]).then_inc(st_out, 16)

        @block.vector
        def _(dve):
            count = [0]

            def link(ins):
                count[0] += 1
                ins.then_inc(v_chain, 1)
                dve.wait_ge(v_chain, count[0])

            TT, TS = nc.vector.tensor_tensor, nc.vector.tensor_scalar

            def lo_of(out, whole, hi):
                return TT(out, whole, hi.bitcast(F32), ALU.subtract)

            def y_lo_of(group, h, c):
                dve.wait_ge(a_yh, KC * group + c + 1)
                lo_of(y_lo[:, c, half(h)], y[:, c, half(h)], y_hi[:, c, half(h)]).then_inc(v_yl, 1)

            nc.vector.memset(idle[:], 0.0).then_inc(v_idle, 1)
            dve.wait_ge(a_l1, 1)
            lo_of(lora1_lo[:], lora1[:], lora1_hi[:]).then_inc(v_l1, 1)

            dve.wait_ge(ld_cb, 16)
            link(TS(c_abs, cbk[:], -1.0, None, ALU.mult))
            link(TT(c_abs, c_abs, cbk[:], ALU.max))
            link(nc.vector.tensor_reduce(cbt[:, 5, 0:1], c_abs, AX_X, ALU.max))
            link(TS(cbt[:, 5, 0:1], cbt[:, 5, 0:1], 1e-8, None, ALU.max))
            link(nc.vector.reciprocal(cbt[:, 5, 1:2], cbt[:, 5, 0:1]))
            link(TS(c_n, cbk[:], cbt[:, 5, 1:2], None, ALU.mult))
            TT(step[:, 0:7], c_n[:, 1:8], c_n[:, 0:7], ALU.subtract)
            link(TT(thr[:, 0:7], c_n[:, 1:8], c_n[:, 0:7], ALU.add))
            link(TS(thr[:, 0:7], thr[:, 0:7], 0.5, None, ALU.mult))
            link(nc.vector.tensor_copy(u[:, 3:4], thr[:, 3:4]))
            TT(u[:, 1:2], thr[:, 1:2], thr[:, 3:4], ALU.min)
            link(TT(u[:, 5:6], thr[:, 5:6], thr[:, 3:4], ALU.max))
            TT(u[:, 0:1], thr[:, 0:1], u[:, 1:2], ALU.min)
            TT(u[:, 6:7], thr[:, 6:7], u[:, 5:6], ALU.max)
            TT(c_abs[:, 2:3], thr[:, 2:3], u[:, 1:2], ALU.max)
            link(TT(c_abs[:, 4:5], thr[:, 4:5], u[:, 3:4], ALU.max))
            TT(u[:, 2:3], c_abs[:, 2:3], u[:, 3:4], ALU.min)
            link(TT(u[:, 4:5], c_abs[:, 4:5], u[:, 5:6], ALU.min))

            dve.wait_ge(a_es, 1)
            nc.vector.reciprocal(rscale[:], scale[:]).then_inc(v_rs, 1)

            def router_bias():
                dve.wait_ge(ld_lang, 16)
                link(nc.vector.tensor_copy(lang_f[:], lang_i[:]))
                dve.wait_ge(ld_c, 16)
                link(TT(bias[:], lang_f[:].unsqueeze(2).to_broadcast([P, NB, E]),
                        e_iota.unsqueeze(1).to_broadcast([P, NB, E]), ALU.is_equal))
                link(TS(bias[:], bias[:], 5.0, None, ALU.mult))

            def router_top2():
                dve.wait_ge(s_hlog, NB // 2)
                lg, eq, sc, oh1, lg2, oh2 = (rt[:, k] for k in range(6))
                m1, m2, first = rs1[:, 0], rs1[:, 1], rs1[:, 4]
                rank = e_rank.unsqueeze(1).to_broadcast([P, NB, E])
                link(TT(lg.rearrange("p (k b) e -> p k b e", b=2), bias[:].rearrange("p (k b) e -> p k b e", b=2),
                        hl[:, :, :, E * R:AW], ALU.add))
                link(nc.vector.tensor_reduce(m1, lg, AX_X, ALU.max))
                for src, m, oh in ((lg, m1, oh1), (lg2, m2, oh2)):
                    if src is lg2:
                        link(nc.vector.scalar_tensor_tensor(lg2, oh1, -3.0e38, lg, ALU.mult, ALU.add))
                        link(nc.vector.tensor_reduce(m2, lg2, AX_X, ALU.max))
                    link(TT(eq, src, wide(m), ALU.is_equal))
                    link(TT(sc, eq, rank, ALU.mult))
                    link(nc.vector.tensor_reduce(first, sc, AX_X, ALU.max))
                    link(TT(oh, rank, wide(first), ALU.is_equal))
                TT(rs1[:, 2], m2, m1, ALU.subtract).then_inc(v_dm, 1)

            hl = ps[:, 4:8, 0:2 * AW].rearrange("p k (b n) -> p k b n", b=2)

            def wide(v):
                return v.unsqueeze(2).to_broadcast([P, NB, E])

            def router_gates():
                oh1, oh2 = rt[:, 3], rt[:, 5]
                gap_exp, total, p1, p2 = rs1[:, 3], rs1[:, 5], rs1[:, 6], rs1[:, 7]
                dve.wait_ge(a_exp, 1)
                link(TS(total, gap_exp, 1.0, 0.5, ALU.add, ALU.mult))
                link(nc.vector.reciprocal(p1, total))
                link(TT(p2, gap_exp, p1, ALU.mult))
                TT(oh1, oh1, wide(p1), ALU.mult)
                link(TT(oh2, oh2, wide(p2), ALU.mult))
                link(TT(gates[:], oh1, oh2, ALU.add))
                for k in range(NB // 2):
                    last = TT(gated[:, 2 * k:2 * k + 2], hl[:, k, :, 0:E * R].rearrange("p b (e r) -> p b e r", e=E),
                              gates[:, 2 * k:2 * k + 2].unsqueeze(3).to_broadcast([P, 2, E, R]), ALU.mult)
                last.then_inc(v_gate, 1)

            def quant_product(k, o):
                n, q = w1n[:, o], w1q[:, o]
                if k == 6:
                    if o == 0:
                        dve.wait_ge(p_n, 1)
                    ins = TS(q, n, u[:, 6:7], step[:, 6:7], ALU.is_gt, ALU.mult)
                else:
                    dve.wait_ge(a_step, quant_order.index((k + 1, o)) + 1)
                    ins = nc.vector.scalar_tensor_tensor(q, n, u[:, k:k + 1], q, ALU.is_gt, ALU.mult)
                if (k, o) in products:
                    ins.then_inc(v_step, 1)
                return ins

            def quant_last(o):
                return nc.vector.scalar_tensor_tensor(w1q[:, o], w1q[:, o], c_n[:, 0:1], w1n[:, o],
                                                      ALU.add, ALU.subtract)

            def gh_split(h):
                dve.wait_ge(a_gh, h + 1)
                lo_of(gh_lo[:, half(h)], ps[:, 4 + h], gh_hi[:, half(h)]).then_inc(v_gh, 1)

            for o in (2, 3):
                dve.wait_ge(s_delta, o + 1)
                TS(delta[:, o], ps[:, o], 0.5, None, ALU.mult).then_inc(v_dc, 1)
            router_bias()
            for c in range(KC):
                y_lo_of(0, 0, c)
            for c in range(KC):
                dve.wait_ge(a_w0, c + 1)
                lo_of(w0_lo[:, c], w0[:, c], w0_hi[:, c]).then_inc(v_w0, 1)
            dve.wait_ge(v_rs, 1)
            dve.wait_ge(ld_w1, 32)
            dve.wait_ge(a_dc, 2)
            link(TT(w1n[:, 1], w1[:, 1], delta[:, 1], ALU.add))
            link(TT(groups(w1n[:, 1]), groups(w1n[:, 1]), by_group(rscale, 1), ALU.mult))
            for k in (6, 5, 4):
                quant_product(k, 0)
                quant_product(k, 1)
            router_top2()
            quant_product(3, 0)
            quant_product(3, 1)
            router_gates()
            for k in (2, 1):
                quant_product(k, 0)
                quant_product(k, 1)
            gh_split(0)
            quant_product(0, 0)
            link(quant_product(0, 1))
            quant_last(0).then_inc(v_q, 1)
            gh_split(1)
            quant_last(1).then_inc(v_q, 1)

            def add_result(done, h, c, bank):
                dve.wait_ge(done, KC * h + c + 1)
                return TT(y[:, c, half(h)], y[:, c, half(h)], ps[:, bank], ALU.add)

            def w1t_split(o):
                dve.wait_ge(a_w1t, o + 1)
                lo_of(w1t_lo[:, o].rearrange("p c n -> p (c n)"), ps[:, o],
                      w1t_hi[:, o].rearrange("p c n -> p (c n)")).then_inc(v_w1t, 1)

            for c in range(KC):
                add_result(s_l0, 0, c, c).then_inc(v_y, 1)
            for k in range(5, 1, -1):
                quant_product(k, 2)
                quant_product(k, 3)
            w1t_split(0)
            quant_product(1, 2)
            quant_product(1, 3)
            w1t_split(1)
            quant_product(0, 3)
            link(quant_product(0, 2))
            quant_last(3).then_inc(v_q, 1)
            link(quant_last(2))
            link(TT(w1q[:, 2], w1q[:, 2], w1n[:, 2], ALU.add))
            link(TT(groups(w1q[:, 2]), groups(w1q[:, 2]), by_group(scale, 2), ALU.mult))
            TT(w1q[:, 2], w1q[:, 2], delta[:, 2], ALU.add).then_inc(v_w, 1)
            add_result(s_l0, 1, 0, 4).then_inc(v_y, 1)
            add_result(s_l0, 1, 1, 5).then_inc(v_y, 1)
            w1t_split(2)
            add_result(s_l0, 1, 2, 6).then_inc(v_y, 1)
            add_result(s_l0, 1, 3, 7).then_inc(v_y, 1)
            w1t_split(3)

            def split_wgu(q, s):
                dve.wait_ge(a_wg, 2 * q + s + 1)
                lo_of(wgu_lo[:, s].rearrange("p u c f -> p (u c f)"), wgu[:, s].rearrange("p u c f -> p (u c f)"),
                      wgu_hi[:, s].rearrange("p u c f -> p (u c f)")).then_inc(v_wg, 1)
                dve.wait_ge(a_bl, 2 * q + s + 1)
                whole = bl[:, s].rearrange("p a u f -> p (a u f)")
                nc.vector.scalar_tensor_tensor(whole, whole.bitcast(F32), minus_b_lo,
                                               blr[:, s].rearrange("p a u f -> p (a u f)"),
                                               ALU.mult, ALU.add).then_inc(v_bl, 1)

            def split_wd(q, s):
                dve.wait_ge(a_wd, 2 * q + s + 1)
                lo_of(wd_lo[:, s], wd[:, s], wd_hi[:, s]).then_inc(v_wd, 1)

            def split_ad(q, s, j, h):
                dve.wait_ge(p_ad, 2 * q + s + 1)
                TT(ad[:, s, :, 1], ad_raw(j, h), ad[:, s, :, 0].bitcast(F32), ALU.subtract).then_inc(v_ad, 1)

            def act_up(q, s):
                n = 2 * q + s
                dve.wait_ge(s_u, n + 1)
                dve.wait_ge(a_silu, n + 1)
                if not (isinstance(q, int) and q == 0):
                    dve.wait_ge(a_ah, n - 1)
                    dve.wait_ge(v_al, n - 1)
                TT(act[:, s], silu_g[:, s], ps[:, UP], ALU.mult).then_inc(v_act, 1)

            def act_split(q, s):
                dve.wait_ge(a_ah, 2 * q + s + 1)
                dve.wait_ge(v_act, 2 * q + s + 1)
                lo_of(act_lo[:, s], act[:, s], act_hi[:, s]).then_inc(v_al, 1)

            def ranks_up(h):
                dve.wait_ge(s_ta, h + 1)
                TT(tm[:], ps[:, SPARE], up_mask, ALU.mult).then_inc(v_tm, 1)
                dve.wait_ge(a_th, h + 1)
                lo_of(t_lo[:], tm[:], t_hi[:]).then_inc(v_tl, 1)

            def ranks_stacked(k, done, count_, bank, factor):
                dve.wait_ge(done, count_)
                nc.vector.scalar_tensor_tensor(tm[:], ps[:, bank], factor, pair_mask, ALU.mult, ALU.mult).then_inc(v_tm, 1)
                dve.wait_ge(a_th, k)
                nc.vector.scalar_tensor_tensor(td[:], t_hi[:].bitcast(F32), minus_t_lo, tm[:],
                                               ALU.mult, ALU.add).then_inc(v_tl, 1)

            for c in range(KC):
                add_result(s_l1, 0, c, c).then_inc(v_y, 1)
            for c in range(KC):
                y_lo_of(4, 0, c)
            add_result(s_l1, 1, 0, 4).then_inc(v_y, 1)
            dve.wait_ge(ld_masks, 16)
            ranks_up(0)
            split_wgu(0, 0)
            add_result(s_l1, 1, 1, 5).then_inc(v_y, 1)
            split_wgu(0, 1)
            add_result(s_l1, 1, 2, 6).then_inc(v_y, 1)
            add_result(s_l1, 1, 3, 7).then_inc(v_y, 1)
            for c in range(KC):
                y_lo_of(5, 1, c)

            def out_result(h, c, bank):
                add_result(s_o3, h, c, bank).then_inc(v_out, 1)

            for h in range(2):
                n0 = NJ * h

                def at(j):
                    return (n0 + j) // 2, (n0 + j) % 2

                split_wd(*at(0))
                split_ad(*at(0), 0, h)
                if h == 1:
                    for c in range(KC):
                        add_result(s_dn, 0, c, DOWN + c).then_inc(v_y, 1)
                act_up(*at(0))
                if h == 1:
                    for c in range(KC):
                        y_lo_of(6, 0, c)
                act_split(*at(0))
                if h == 0:
                    dve.wait_ge(ld_t[0], STACK_PARTS)
                    dve.wait_ge(ld_t[1], STACK_PARTS)
                    ranks_up(1)
                split_wgu(*at(2))
                split_wd(*at(1))
                split_ad(*at(1), 1, h)
                act_up(*at(1))
                act_split(*at(1))
                if h == 1:
                    ranks_stacked(4, s_t3, 1, SPARE, 2.0)
                split_wgu(*at(3))
                split_wd(*at(2))
                split_ad(*at(2), 2, h)
                if h == 1:
                    out_result(0, 0, SPARE)
                act_up(*at(2))
                if h == 1:
                    out_result(0, 1, SPARE)
                act_split(*at(2))
                if h == 1:
                    out_result(0, 2, SPARE)
                split_wgu(*at(4))
                with dve.Fori(0, 3) as i:
                    for k in range(2):
                        q, s = at(3 + k)
                        split_wd(q + i, s)
                        split_ad(q + i, s, 3 + k + 2 * i, h)
                        act_up(q + i, s)
                        act_split(q + i, s)
                        split_wgu(q + i + 1, s)
                for j in (9, 10):
                    split_wd(*at(j))
                    split_ad(*at(j), j, h)
                    act_up(*at(j))
                    act_split(*at(j))
                    if h == 0:
                        split_wgu(*at(j + 2))
                if h == 1:
                    out_result(0, 3, SPARE)
                ranks_stacked(3 + 2 * h, s_td, h + 1, TDOWN, 1.0)
            for c in range(KC):
                dve.wait_ge(a_dn, c + 1)
                lo_of(dn_lo[:, c], ps[:, DOWN + c], dn_hi[:, c]).then_inc(v_dn, 1)
            ranks_stacked(6, s_t3, 2, SPARE, 2.0)
            for o, bank in ((1, UP), (3, DOWN)):
                dve.wait_ge(s_o3, KC + o + 1)
                TT(y[:, o, half(1)], y[:, o, half(1)], ps[:, bank], ALU.add).then_inc(v_out, 1)

        @block.gpsimd
        def _(pool):
            count = [0]

            def link(ins):
                count[0] += 1
                ins.then_inc(p_chain, 1)
                pool.wait_ge(p_chain, count[0])

            TT, copy = nc.gpsimd.tensor_tensor, nc.gpsimd.tensor_copy

            pool.wait_ge(ld_w1, 32)
            for o in (0, 2, 3):
                if o == 0:
                    pool.wait_ge(a_dc, 1)
                else:
                    pool.wait_ge(v_dc, o - 1)
                link(TT(w1n[:, o], w1[:, o], delta[:, o], ALU.add))
                if o == 0:
                    pool.wait_ge(v_rs, 1)
                TT(groups(w1n[:, o]), groups(w1n[:, o]), by_group(rscale, o), ALU.mult).then_inc(p_n, 1)

            def y_lo_of(version, h, c):
                pool.wait_ge(a_yh, KC * version + c + 1)
                TT(y_lo[:, c, half(h)], y[:, c, half(h)], y_hi[:, c, half(h)].bitcast(F32),
                   ALU.subtract).then_inc(p_yl, 1)

            def y_lo_half(version, h):
                for c in range(KC):
                    y_lo_of(version, h, c)

            y_lo_half(1, 1)
            pool.wait_ge(a_b0, 1)
            TT(b0_lo[:], b0[:], b0_hi[:].bitcast(F32), ALU.subtract).then_inc(p_b0, 1)
            pool.wait_ge(p_n, KC - 1)
            for o in (2, 3):
                nc.gpsimd.tensor_scalar(w1q[:, o], w1n[:, o], u[:, 6:7], step[:, 6:7], ALU.is_gt,
                                        ALU.mult).then_inc(p_step, 1)
            for o in (0, 1, 3):
                if o == 3:
                    y_lo_half(2, 0)
                pool.wait_ge(v_q, min(o, 2) + 1)
                link(TT(w1q[:, o], w1q[:, o], w1n[:, o], ALU.add))
                link(TT(groups(w1q[:, o]), groups(w1q[:, o]), by_group(scale, o), ALU.mult))
                TT(w1q[:, o], w1q[:, o], delta[:, o], ALU.add).then_inc(p_w, 1)

            def split(pairs, done):
                for hi, lo, raw in pairs:
                    last = copy(hi, raw)
                link(last)
                for hi, lo, raw in pairs:
                    last = TT(lo, raw, hi.bitcast(F32), ALU.subtract)
                last.then_inc(done, 1)

            def split_ag(h):
                pool.wait_ge(ld_ag, 16 * NB)
                split([(ag[:, b // 2, :, :, b % 2, 0], ag[:, b // 2, :, :, b % 2, 1], agr[:, b])
                       for b in range(HB * h, HB * (h + 1))], p_ag)

            def split_b3(h):
                for b in range(HB * h, HB * (h + 1)):
                    raw = b3r[:, b]
                    for g in (2, 3):
                        copy(b3[:, :, b, g], raw)
                    link(copy(b3[:, :, b, 0], raw))
                    last = TT(b3[:, :, b, 1], raw, b3[:, :, b, 0].bitcast(F32), ALU.subtract)
                last.then_inc(p_b3, 1)

            def stack_b(h, p, dst, raw, ld, done):
                pool.wait_ge(ld, 16 * HB * (h + 1))
                out = dst[:, 2 * h + p]
                link(copy(out, raw[:, p]))
                link(nc.gpsimd.tensor_scalar(b_part[:], out.bitcast(F32), minus_b_lo, None, ALU.mult))
                TT(out, raw[:, p], b_part[:], ALU.add).then_inc(done, 1)
                pool.wait_ge(done, 2 * h + p + 1)

            def split_ad(q, s, j, h):
                pool.wait_ge(ld_ad, 16 * NB)
                if not (isinstance(q, int) and q == 0):
                    pool.wait_ge(s_d, 2 * q + s - 1)
                copy(ad[:, s, :, 0], ad_raw(j, h))
                copy(ad[:, s, :, 2], ad_raw(j, h))
                copy(ad[:, s, :, 3], ad_raw(j, h)).then_inc(p_ad, 1)

            y_lo_half(3, 1)
            split_ag(0)
            split_ag(1)
            pool.wait_ge(s_w1t, KC)
            for h in range(2):
                n0 = NJ * h

                def at(j):
                    return (n0 + j) // 2, (n0 + j) % 2

                split_ad(*at(0), 0, h)
                split_ad(*at(1), 1, h)
                if h == 0:
                    stack_b(0, 0, bd, bdr, ld_bd, p_bd)
                    stack_b(0, 1, bd, bdr, ld_bd, p_bd)
                split_ad(*at(2), 2, h)
                if h == 0:
                    stack_b(0, 0, a3, a3r, ld_a3, p_a3)
                    stack_b(0, 1, a3, a3r, ld_a3, p_a3)
                for j in range(3, 7):
                    split_ad(*at(j), j, h)
                    if h == 1:
                        if j < 5:
                            stack_b(1, j - 3, bd, bdr, ld_bd, p_bd)
                        else:
                            stack_b(1, j - 5, a3, a3r, ld_a3, p_a3)
                    elif j < 5:
                        if j == 3:
                            pool.wait_ge(ld_b3, 16 * NB)
                            pool.wait_ge(s_l0, 2 * KC)
                        split_b3(j - 3)
                with pool.Fori(0, 2) as i:
                    for k in range(2):
                        q, s = at(7 + k)
                        split_ad(q + i, s, 7 + k + 2 * i, h)


def kernel(**inputs):
    import numpy as np
    import concourse.bacc as bacc
    from concourse import mybir as mb
    from concourse.bass_utils import run_bass_kernel_spmd as run

    a = {k: np.asarray(v) for k, v in inputs.items()}

    def pad_f(m, axis):
        width = [(0, 0)] * m.ndim
        width[axis] = (0, FP - F)
        return np.pad(m, width)

    def gate_up(wg, wu):
        w = np.stack([pad_f(wg, 0), pad_f(wu, 0)])
        return w.reshape(2, NJ, P, KC, P).transpose(1, 4, 0, 3, 2).reshape(NJ, P, 2 * KC * P)

    row, col = np.arange(P)[:, None], np.arange(H)[None]
    consts = np.concatenate([
        np.eye(P), np.arange(E) + 0 * row, E - np.arange(E) + 0 * row, -1.0 * (row // R % G4 == 2),
        -1.0 * (row // R % G4 == 3), 0.5 * (row // (2 * R) % 2 == col // BT % 2),
        0.5 * (row // (G4 * R) == col // BT % 2)], axis=1).astype(np.float32)
    na = a["L2_cond_A_gate"].shape[1]
    ag = np.stack([a["L2_cond_A_gate"][0], a["L2_cond_A_up"][0]])
    bg = np.stack([pad_f(a["L2_cond_B_gate"][0], 1), pad_f(a["L2_cond_B_up"][0], 1)])
    adn = pad_f(a["L2_cond_A_down"][0], 2)
    arrays = {
        "x": a["x"].reshape(TOK, D).T,
        "aw": np.concatenate([a["L0_cond_A"].reshape(E * R, D), a["L0_cond_Wr"]]).T,
        "w0": a["L0_cond_W"].T,
        "b0": a["L0_cond_B"].transpose(0, 2, 1).reshape(E * R, D),
        "w1": a["L1_cond_weight"],
        "slog": a["L1_cond_scale_log"].reshape(D, KC),
        "lora1": np.concatenate([a["L1_cond_lora_B"].T, a["L1_cond_lora_A"]], axis=1),
        "cb": a["condB_codebook"],
        "lang": a["itok_B_0_7"],
        "idx2": a["itok_B_2_6"].reshape(1, NB),
        "idx3": a["itok_B_3_7"].reshape(1, NB),
        "wgu": gate_up(a["L2_cond_W_gate"], a["L2_cond_W_up"]),
        "wd": pad_f(a["L2_cond_W_down"], 1).T.reshape(NJ, P, D),
        "agu": ag.reshape(2, na, R, KC, P).transpose(1, 4, 3, 0, 2).reshape(na, P, KC * 2 * R),
        "bgu": bg.reshape(2, na, NJ, P, R).transpose(1, 2, 4, 0, 3).reshape(na, NJ, R, 2 * P),
        "ad": adn.reshape(na, R, NJ, P).transpose(0, 3, 2, 1).reshape(na, P, NJ * R),
        "bd": a["L2_cond_B_down"][0].transpose(0, 2, 1),
        "a3": a["L3_cond_A"].transpose(0, 2, 1),
        "b3": a["L3_cond_B"].reshape(-1, R, KC, P).transpose(0, 3, 2, 1).reshape(-1, P, KC * R),
        "consts": consts,
    }
    nc = bacc.Bacc("TRN2", target_bir_lowering=False, num_devices=1)
    feeds, aps = {}, {}
    for name, v in arrays.items():
        v = np.ascontiguousarray(v)
        feeds[name + "_dram"] = v
        aps[name] = nc.dram_tensor(name + "_dram", v.shape, mb.dt.from_np(v.dtype), kind="ExternalInput").ap()
    aps["out"] = nc.dram_tensor("out_dram", (D, TOK), mb.dt.float32, kind="ExternalOutput").ap()
    program(nc, aps)
    r = run(nc, [feeds], core_ids=[0])
    return np.ascontiguousarray(r.results[0]["out_dram"].T).reshape(NB, BT, D)
```
